# Optimizing a Trainium2 kernel written in Bass

```python
import numpy as np
import jax
import jax.numpy as jnp

def _softmax(x, axis=-1):
    return jax.nn.softmax(x, axis=axis)

def _gelu(x):
    return jax.nn.gelu(x, approximate=True)

def _silu(x):
    return jax.nn.silu(x)

def _sigmoid(x):
    return jax.nn.sigmoid(x)

def _layernorm(x, axis=-1, eps=1e-05):
    m = jnp.mean(x, axis=axis, keepdims=True)
    v = jnp.var(x, axis=axis, keepdims=True)
    return (x - m) / jnp.sqrt(v + eps)

def _scatter_add(tgt, idx, src, axis=0):
    return tgt.at[idx].add(src)

def _segment_sum(src, seg, n):
    return jax.ops.segment_sum(src, seg, n)
kernel_name = 'mk_gnn_resnorm_d1_gnn_r8_7ff9af'

def setup_inputs(seed: int=0):
    np.random.seed(seed)
    _w = jnp.asarray

    def _rec_inputs():
        import jax
        import jax.numpy as jnp
        _gk = jax.random.key(seed)
        x = -0.0002221 + 1 * jax.random.normal(jax.random.fold_in(_gk, 1), (1250, 768), jnp.float32)
        src = jax.random.randint(jax.random.fold_in(_gk, 2), (40000,), 0, 1250, jnp.int32)
        dst = jax.random.randint(jax.random.fold_in(_gk, 3), (40000,), 0, 1250, jnp.int32)
        _o = jnp.argsort(dst, stable=True)
        src = src[_o]
        dst = dst[_o]
        edge_type_3 = jax.random.randint(jax.random.fold_in(_gk, 12), (40000,), 0, 3, jnp.int32)
        return (x, src, dst, edge_type_3)
    x, src, dst, edge_type_3 = _rec_inputs()

    def _L0_gnn_setup():
        import jax, jax.numpy as jnp
        import numpy as np
        NEG_SLOPE = 0.2
        EPS = 1e-16
        N_NODES = 4096
        N_EDGES = 20000
        DIM = 768
        HEADS1 = 4
        OUT1 = DIM // HEADS1
        HEADS2 = 1
        OUT2 = DIM
        N_REL = 3

        def rgat_conv(x, W, q, k, b, src, dst, etype, heads, out_ch, n_nodes):
            xr = jnp.einsum('nd,rdf->rnf', x, W)
            oi = xr[etype, dst]
            oj = xr[etype, src]
            qi = oi @ q
            kj = oj @ k
            alpha = jax.nn.leaky_relu(qi + kj, NEG_SLOPE)
            m = jax.ops.segment_max(alpha, dst, num_segments=n_nodes)
            e = jnp.exp(alpha - m[dst])
            z = jax.ops.segment_sum(e, dst, num_segments=n_nodes)
            a = e / (z[dst] + EPS)
            msg = (a[:, :, None] * oj.reshape(-1, heads, out_ch)).reshape(-1, heads * out_ch)
            out = jax.ops.segment_sum(msg, dst, num_segments=n_nodes)
            return out + b
        key = jax.random.key(seed)
        ks = jax.random.split(key, 12)
        s = 0.02
        return {'x': jax.random.normal(ks[0], (N_NODES, DIM), dtype=jnp.float32), 'edge_index': jax.random.randint(ks[1], (2, N_EDGES), 0, N_NODES, dtype=jnp.int64), 'edge_type': jax.random.randint(ks[2], (N_EDGES,), 0, N_REL, dtype=jnp.int64), 'W1': jax.random.normal(ks[3], (N_REL, DIM, HEADS1 * OUT1), dtype=jnp.float32) * s, 'q1': jax.random.normal(ks[4], (HEADS1 * OUT1, HEADS1), dtype=jnp.float32) * s, 'k1': jax.random.normal(ks[5], (HEADS1 * OUT1, HEADS1), dtype=jnp.float32) * s, 'b1': jnp.zeros((HEADS1 * OUT1,), dtype=jnp.float32), 'W2': jax.random.normal(ks[6], (N_REL, DIM, HEADS2 * OUT2), dtype=jnp.float32) * s, 'q2': jax.random.normal(ks[7], (HEADS2 * OUT2, HEADS2), dtype=jnp.float32) * s, 'k2': jax.random.normal(ks[8], (HEADS2 * OUT2, HEADS2), dtype=jnp.float32) * s, 'b2': jnp.zeros((HEADS2 * OUT2,), dtype=jnp.float32)}
    _L0_gnn_all = _L0_gnn_setup()
    _L0_gnn_in = {k: v for k, v in _L0_gnn_all.items() if k in ('W1', 'q1', 'k1', 'b1', 'W2', 'q2', 'k2', 'b2')}
    del _L0_gnn_all
    return {'x': x, 'src': src, 'dst': dst, 'edge_type_3': edge_type_3, 'L0_gnn_W1': _L0_gnn_in['W1'], 'L0_gnn_q1': _L0_gnn_in['q1'], 'L0_gnn_k1': _L0_gnn_in['k1'], 'L0_gnn_b1': _L0_gnn_in['b1'], 'L0_gnn_W2': _L0_gnn_in['W2'], 'L0_gnn_q2': _L0_gnn_in['q2'], 'L0_gnn_k2': _L0_gnn_in['k2'], 'L0_gnn_b2': _L0_gnn_in['b2']}

def reference(x, src, dst, edge_type_3, L0_gnn_W1, L0_gnn_q1, L0_gnn_k1, L0_gnn_b1, L0_gnn_W2, L0_gnn_q2, L0_gnn_k2, L0_gnn_b2):
    import jax
    import jax.numpy as jnp

    def _L0_gnn_ref(x, edge_index, edge_type, W1, q1, k1, b1, W2, q2, k2, b2):
        import jax, jax.numpy as jnp
        import numpy as np
        NEG_SLOPE = 0.2
        EPS = 1e-16
        N_NODES = 4096
        N_EDGES = 20000
        DIM = 768
        HEADS1 = 4
        OUT1 = DIM // HEADS1
        HEADS2 = 1
        OUT2 = DIM
        N_REL = 3

        def rgat_conv(x, W, q, k, b, src, dst, etype, heads, out_ch, n_nodes):
            xr = jnp.einsum('nd,rdf->rnf', x, W)
            oi = xr[etype, dst]
            oj = xr[etype, src]
            qi = oi @ q
            kj = oj @ k
            alpha = jax.nn.leaky_relu(qi + kj, NEG_SLOPE)
            m = jax.ops.segment_max(alpha, dst, num_segments=n_nodes)
            e = jnp.exp(alpha - m[dst])
            z = jax.ops.segment_sum(e, dst, num_segments=n_nodes)
            a = e / (z[dst] + EPS)
            msg = (a[:, :, None] * oj.reshape(-1, heads, out_ch)).reshape(-1, heads * out_ch)
            out = jax.ops.segment_sum(msg, dst, num_segments=n_nodes)
            return out + b
        src, dst = (edge_index[0], edge_index[1])
        n = x.shape[0]
        h = rgat_conv(x, W1, q1, k1, b1, src, dst, edge_type, HEADS1, OUT1, n)
        h = jax.nn.elu(h)
        out = rgat_conv(h, W2, q2, k2, b2, src, dst, edge_type, HEADS2, OUT2, n)
        return out
    edge_index = jnp.stack([src, dst])
    x = _layernorm(x + _L0_gnn_ref(x, edge_index, edge_type_3, L0_gnn_W1, L0_gnn_q1, L0_gnn_k1, L0_gnn_b1, L0_gnn_W2, L0_gnn_q2, L0_gnn_k2, L0_gnn_b2), axis=-1)
    return x

_drawn_inputs = setup_inputs


def setup_inputs(seed=0):
    import zlib

    import numpy as np

    out = dict(_drawn_inputs(seed))
    spreads = {'L0_gnn_b1': (0.0, 0.1), 'L0_gnn_b2': (0.0, 0.1)}
    factors = {'L0_gnn_W1': 5.506, 'L0_gnn_q1': 8.0, 'L0_gnn_k1': 8.0, 'L0_gnn_q2': 8.0, 'L0_gnn_k2': 8.0}
    for name, (base, spread) in spreads.items():
        noise = np.random.default_rng([zlib.crc32(name.encode()), seed]).standard_normal(out[name].shape)
        drawn = base * np.exp(spread * noise) if base else spread * noise
        out[name] = jnp.asarray(drawn.astype(out[name].dtype))
    for name, factor in factors.items():
        out[name] = (out[name] * factor).astype(out[name].dtype)
    return out
```

```python
from contextlib import ExitStack

import concourse.bass as bass
from concourse import mybir

P = 128
F32 = mybir.dt.float32
BF16 = mybir.dt.bfloat16
I32 = mybir.dt.int32
U32 = mybir.dt.uint32
U16 = mybir.dt.uint16
ALU = mybir.AluOpType
ACT = mybir.ActivationFunctionType
AX = mybir.AxisListType.X

SLOPE = 0.2
Z_EPS = 1e-16
LN_EPS = 1e-5
BIG = 1e30
CODE_DST = 8192
CODE_TYPE = 2048
WIN = 8
RUN = 3
GRAN = 32


def rgat(nc, x, src, dst, etype, W1, q1, k1, b1, W2, q2, k2, b2, out):
    N, F = x.shape
    E = src.shape[0]
    R = W1.shape[0]
    H = q1.shape[1]
    HD = F // H
    KT = F // P
    NT = (N + P - 1) // P
    NP = NT * P
    TAIL = N - (NT - 1) * P
    RS = R * NT
    HP = H // 2
    QC = 2 * R * H
    QC2 = 2 * R
    HF = F // 2
    EP = 125
    EC = E // EP
    NW = NP // WIN
    SW = NW // 2
    WM = RS * WIN
    RUNL = RUN * P
    NROW = E // GRAN
    PADL = RUNL
    XB = 2 * (HD + 1)
    DH = NP // 2
    DT = NT // 2
    XW = F + 1
    assert EP * EC == E and R == 3 and H == 4 and WM * 2 <= 512 and NW <= 2 * P and HD * 2 == HF

    code_d = nc.dram_tensor("code_d", [E + PADL], F32).ap()
    runs_d = nc.dram_tensor("runs_d", [NROW, RUNL], F32).ap()
    xr_d = nc.dram_tensor("xr_d", [RS, 2, P, XB], F32).ap()
    xr2_d = nc.dram_tensor("xr2_d", [RS, P, XW], F32).ap()
    ab_d = nc.dram_tensor("ab_d", [QC, NP], F32).ap()
    ab2_d = nc.dram_tensor("ab2_d", [QC2, NP], F32).ap()

    with ExitStack() as ctx:
        def sb(name, shape, dt=F32):
            return ctx.enter_context(nc.sbuf_tensor(name, shape, dt))

        def sem(name):
            return ctx.enter_context(nc.semaphore(name))

        Ct = sb("Ct", [P, RS, NP], U16)
        xT = sb("xT", [P, KT, NP])
        ident = sb("ident", [P, P])
        onesf = sb("onesf", [P, 2])
        zm = sb("zm", [P, 512], BF16)
        i_m = sb("i_m", [P, WM], BF16)
        i_s = sb("i_s", [P, P], BF16)
        qv1 = sb("qv1", [P, KT, 2 * H])
        qv2 = sb("qv2", [P, KT, 2])
        wqk1 = sb("wqk1", [P, KT, QC])
        wqk2 = sb("wqk2", [P, KT, QC2])
        qk1t = sb("qk1t", [P, NT, QC])
        ks1 = sb("ks1", [P, NT, R * H])
        qk2t = sb("qk2t", [P, NT, QC2])
        ks2 = sb("ks2", [P, NT, R])
        mk1 = sb("mk1", [P, NT, R, H])
        mk2 = sb("mk2", [P, NT, R, 1])
        mx1 = sb("mx1", [P, 4, NT, H])
        mx2 = sb("mx2", [P, 4, NT, 1])
        ab1 = sb("ab1", [P, NT, QC])
        ab2 = sb("ab2", [P, NT, QC2])
        b1b = sb("b1b", [P, F])
        b2b = sb("b2b", [P, F])
        code = sb("code", [P, EC])
        small = sb("small", [P, 64])
        smalli = sb("smalli", [P, 8], U32)
        ARENA = 22432
        ar = sb("arena", [P, ARENA])
        ps = [ctx.enter_context(nc.psum_tensor(f"ps{i}", [P, 512], F32)) for i in range(8)]

        def cut(at, n):
            assert at + n <= ARENA, (at, n)
            return ar[:, at:at + n]

        WS = KT * F
        wslot = [cut(i * WS, WS).rearrange("p (k f) -> p k f", k=KT) for i in range(2)]
        pos = [2 * WS]

        def take(n):
            pos[0] += n
            return cut(pos[0] - n, n)

        dsti, srci, eti = (take(EC).bitcast(I32) for _ in range(3))
        tmpf = take(EC)
        rowb = take(2 * EC).rearrange("p (s c) -> p s c", s=2)
        runb = take(2 * RUNL).rearrange("p (s c) -> p s c", s=2)
        NE = 2 * RUN * SW
        edi = take(NE).bitcast(I32)
        u0, u1 = take(NE).bitcast(I32), take(NE).bitcast(I32)
        f0, f1 = take(NE), take(NE)
        wid = take(NE)
        wrow = take(NW)
        G = take(NW)
        slo = take(NE)
        mcode = take(NE)
        NOH = 4 * RUN
        oh_s = take(NOH * P // 2).bitcast(BF16).rearrange("p (n s) -> p n s", n=NOH)
        ohs = [oh_s[:, i, :] for i in range(NOH)]
        own6 = [small[:, 44 + h * 6:50 + h * 6].rearrange("p (t c) -> p t c", c=2) for h in range(2)]
        sls = slo.rearrange("p (s t w) -> p s t w", s=2, t=RUN)
        ohm = [take(WM // 2).bitcast(BF16) for _ in range(NOH)]
        x_sb = Ct[:, :, :].rearrange("p a b -> p (a b)")[:, 0:2 * NT * F].bitcast(F32).rearrange("p (t f) -> p t f", t=NT)
        pos[0] = 2 * WS
        Mk = [take(H * NP).rearrange("p (h d) -> p h d", h=H) for _ in range(2)]
        cneg = [take(NP // 2).bitcast(BF16) for _ in range(2)]
        stg = [take(2 * XB) for _ in range(2)]
        WT = [s[:, 0:F] for s in stg]
        stg1 = [s.rearrange("p (a c) -> p a c", a=2) for s in stg]
        rows = Mk[0][:, 0, :]
        pos[0] = 0
        NX = 5
        abr = take(R * 4 * DH).rearrange("p (r c d) -> p r c d", r=R, c=4)
        e1 = [take(2 * DH).rearrange("p (h d) -> p h d", h=2) for _ in range(5)]
        e2 = [take(2 * DH).rearrange("p (h d) -> p h d", h=2) for _ in range(2)]
        xring = [take(XB) for _ in range(NX)]
        hst = take(DT * HF).rearrange("p (t f) -> p t f", t=DT)
        hmn = take(DT * HF).rearrange("p (t f) -> p t f", t=DT)
        pos[0] = 0
        ab2r = take(R * 2 * 512).rearrange("p (r c d) -> p r c d", r=R, c=2)
        g1 = [take(512) for _ in range(5)]
        g2 = [take(512) for _ in range(2)]
        x2ring = [take(XW + 1) for _ in range(NX)]
        GT = 4
        ost = take(GT * F).rearrange("p (t f) -> p t f", t=GT)
        xres = take(GT * F).rearrange("p (t f) -> p t f", t=GT)
        st6 = take(GT * 12).rearrange("p (t s) -> p t s", t=GT)
        mv = take(GT * 2).rearrange("p (t s) -> p t s", t=GT)

        names = """edges_in x_in qv_in bias_in consts x_zero code_ready pad_ready code_out runs_out ranks row_ready
        rows_in off_ready runs_in run_tr ed_ready flag_sum flag_tot flag_ready x_tr xt_ready wt_tr wt_ready wq_done
        wq_ready qk_done qk_ready oh_m oh_s oh_used c_done c_ready fb_built fb_used fb_done fb_free fb_c fb_evac
        t_done t_evac ones_in mk_step mk_cneg mk_ready mk_tr mk_red ab_ready ab_tr ab_rows ab_out
        e_ready e_max e2_free a_ready a_used g_done g_free h_lin h_exp h_ready h_tr ht_ready ht_free
        o_var o_std o_ready o_out chain pool_ready own_in own_seen""".split()
        S = {n: sem(n) for n in names}
        w_in = [sem(f"w_in{i}") for i in range(2)]
        xr_out = [sem(f"xr_out{i}") for i in range(2)]
        xr_in = [sem(f"xr_in{i}") for i in range(NX)]
        ab_in = [sem(f"ab_in{i}") for i in range(R)]
        xres_in = sem("xres_in")

        class Layer:
            pass

        def layer(H, qv, wqk, qk, ks, mk, mx, ab, C, abd, n):
            v = Layer()
            v.H, v.qv, v.wqk, v.qk, v.ks, v.mk, v.mx, v.ab, v.C, v.abd, v.n = H, qv, wqk, qk, ks, mk, mx, ab, C, abd, n
            v.units = [[(r, h) for h in range(H)] for r in range(R)] if H > 1 else [[(r, 0) for r in range(R)]]
            return v

        L1 = layer(H, qv1, wqk1, qk1t, ks1, mk1, mx1, ab1, QC, ab_d, 0)
        L2 = layer(1, qv2, wqk2, qk2t, ks2, mk2, mx2, ab2, QC2, ab2_d, 1)
        WOFF = [0, 3, 6, 9]
        GROUPS = [(0, 3), (3, 6), (6, 10)]
        NG1 = 4
        NST = NG1 * RS
        RING = NX
        NB_X = 3 * KT

        def group1(g):
            return g % 2, g // 2

        def store_out(sp, g):
            t0, t1 = GROUPS[g]
            for t in range(t0, t1):
                m = TAIL if t == NT - 1 else P
                sp.wait_ge(S["o_ready"], t + 1)
                sp.dma_start(out[t * P:t * P + m, :], ost[0:m, t - t0, :]).then_inc(S["o_out"], 16)

        def used(n):
            lay, r = n // 6, n % 3
            if n % 6 < 3:
                return S["wq_done"], (lay * R + r + 1) * KT
            return S["t_done"], (lay * R + r + 1) * NT

        block = ctx.enter_context(nc.Block())

        @block.sync
        def _(sp):
            for t, a in ((dsti, dst), (srci, src), (eti, etype)):
                sp.dma_start(t[0:EP, :], a.rearrange("(p c) -> p c", p=EP)).then_inc(S["edges_in"], 16)
            sp.wait_ge(S["x_zero"], 1)
            sp.dma_start(x_sb[:, 0:NT - 1, :], x[0:(NT - 1) * P, :].rearrange("(t p) f -> p t f", p=P)).then_inc(S["x_in"], 16)
            sp.dma_start(x_sb[0:TAIL, NT - 1, :], x[(NT - 1) * P:N, :]).then_inc(S["x_in"], 16)
            for q, k, t in ((q1, k1, qv1), (q2, k2, qv2)):
                h = t.shape[2] // 2
                sp.dma_start(t[:, :, 0:h], q.rearrange("(k p) h -> p k h", p=P), allow_slow_non_contiguous=True).then_inc(S["qv_in"], 16)
                sp.dma_start(t[:, :, h:2 * h], k.rearrange("(k p) h -> p k h", p=P), allow_slow_non_contiguous=True).then_inc(S["qv_in"], 16)

            def load_w(n):
                if n >= 2:
                    sp.wait_ge(*used(n - 2))
                w = (W1, W1, W2, W2)[n // 3][n % 3]
                sp.dma_start(wslot[n % 2], w.rearrange("(k p) f -> p k f", p=P)).then_inc(w_in[n % 2], 16)

            load_w(0)
            load_w(1)
            for t, a in ((b1b, b1), (b2b, b2)):
                sp.dma_start(t[:, :], a.rearrange("(a f) -> a f", a=1).broadcast_to([P, F])).then_inc(S["bias_in"], 16)
            sp.wait_ge(S["code_ready"], 1)
            sp.dma_start(code_d[0:E].rearrange("(p c) -> p c", p=EP), code[0:EP, :]).then_inc(S["code_out"], 16)
            sp.dma_start(code_d[E:E + PADL].rearrange("(a c) -> a c", a=1), f1[0:1, 0:PADL]).then_inc(S["code_out"], 16)
            sp.wait_ge(S["code_out"], 32)
            every = bass.AP(code_d.tensor, 0, [[GRAN, NROW], [1, RUNL]])
            sp.dma_start(runs_d[:, :], every).then_inc(S["runs_out"], 16)
            for n in range(2, 5):
                load_w(n)

            def store_xr(lay):
                for n in range(RS):
                    sp.wait_ge(S["t_evac"], lay.n * RS + n + 1)
                    if lay is L1:
                        sp.dma_start(xr_d[n].rearrange("a p c -> p a c"), stg1[n % 2]).then_inc(xr_out[n % 2], 16)
                    else:
                        sp.dma_start(xr2_d[n], stg[n % 2][:, 0:XW]).then_inc(xr_out[n % 2], 16)
                    if n % NT == NT - 1:
                        if lay is L1:
                            load_w(5 + n // NT)
                        elif n == NT - 1:
                            load_w(11)

            def ab_store(lay):
                sp.wait_ge(S["ab_rows"], lay.n + 1)
                sp.dma_start(lay.abd[:, :], rows[0:lay.C, :]).then_inc(S["ab_out"], 16)
                sp.wait_ge(S["ab_out"], 16 * (lay.n + 1))
                for i in range(2):
                    sp.wait_ge(xr_out[i], 16 * (lay.n + 1) * RS // 2)

            store_xr(L1)
            load_w(8)
            ab_store(L1)
            sp.wait_ge(*used(8))

            def load_ab1(g, r):
                hp, dh = group1(g)
                c = r * 8 + hp * 4
                sp.dma_start(abr[:, r, :, :], ab_d[c:c + 4, dh * DH:(dh + 1) * DH].partition_broadcast(P)).then_inc(ab_in[r], 16)

            for r in range(R):
                load_ab1(0, r)
            for g in range(NG1):
                hp, dh = group1(g)
                for r in range(R):
                    with sp.Fori(0, NT // NX) as j:
                        for i in range(NX):
                            sp.wait_ge(S["a_used"], j * NX + ((g * R + r) * NT + i + 1))
                            sp.dma_start(xring[i], xr_d[bass.ds(j * NX + (r * NT + i), 1), hp].squeeze(0)).then_inc(xr_in[i], 16)
                    if g + 1 < NG1:
                        sp.wait_ge(S["e_ready"], (g * R + r + 1) * NT)
                        load_ab1(g + 1, r)
            sp.wait_ge(S["h_tr"], 3 * NG1)
            load_w(9)
            load_w(10)
            store_xr(L2)
            ab_store(L2)
            sp.wait_ge(*used(11))

            def load_ab2(g, r):
                t0, t1 = GROUPS[g]
                w = (t1 - t0) * P
                sp.dma_start(ab2r[:, r, :, 0:w], ab2_d[r * 2:r * 2 + 2, t0 * P:t1 * P].partition_broadcast(P)).then_inc(ab_in[r], 16)

            for r in range(R):
                load_ab2(0, r)
            for g, (t0, t1) in enumerate(GROUPS):
                for r in range(R):
                    with sp.Fori(0, NT // NX) as j:
                        for i in range(NX):
                            sp.wait_ge(S["a_used"], j * NX + (NST + (g * R + r) * NT + i + 1))
                            sp.dma_start(x2ring[i][:, 0:XW], xr2_d[bass.ds(j * NX + (r * NT + i), 1)].squeeze(0)).then_inc(xr_in[i], 16)
                    if g + 1 < len(GROUPS):
                        sp.wait_ge(S["e_ready"], NST + (g * R + r + 1) * NT)
                        load_ab2(g + 1, r)
                    if r == 1:
                        if g:
                            store_out(sp, g - 1)
                            sp.wait_ge(S["o_out"], 16 * t0)
                        for t in range(t0, t1):
                            m = TAIL if t == NT - 1 else P
                            sp.dma_start(xres[0:m, t - t0, :], x[t * P:t * P + m, :]).then_inc(xres_in, 16)
            store_out(sp, len(GROUPS) - 1)
            sp.wait_ge(S["o_out"], 16 * NT)

        @block.gpsimd
        def _(pool):
            nc.gpsimd.memset(ident[:, :], 0.0).then_inc(S["pool_ready"], 1)
            pool.wait_ge(S["pool_ready"], 1)
            io = dict(allow_small_or_imprecise_dtypes=True)
            nc.gpsimd.affine_select(out=ident[:, :], in_=ident[:, :], compare_op=ALU.not_equal, fill=1.0,
                                    base=0, pattern=[[-1, P]], channel_multiplier=1).then_inc(S["consts"], 1)
            nc.gpsimd.iota(wrow, [[1, NW]], base=0, channel_multiplier=0, **io).then_inc(S["consts"], 1)
            nc.gpsimd.iota(small[:, 0:2], [[SW, 2]], base=0, channel_multiplier=1, **io).then_inc(S["consts"], 1)
            nc.gpsimd.memset(onesf[:, :], 1.0).then_inc(S["consts"], 1)
            nc.gpsimd.iota(wid, [[SW, 2], [0, RUN], [1, SW]], base=0, channel_multiplier=0, **io).then_inc(S["consts"], 1)
            nc.gpsimd.iota(i_m[:, :], [[1, WM]], base=0, channel_multiplier=0, **io).then_inc(S["consts"], 1)
            nc.gpsimd.iota(i_s[:, :], [[1, P]], base=0, channel_multiplier=0, **io).then_inc(S["consts"], 1)
            nc.gpsimd.memset(zm[:, :], 0.0).then_inc(S["consts"], 1)
            pool.wait_ge(S["code_out"], 32)
            pool.wait_ge(S["row_ready"], 1)
            for s in range(2):
                nc.gpsimd.indirect_dma_start(rowb[0:SW, s, :], None, code_d[0:E].rearrange("(p c) -> p c", c=EC),
                                             bass.IndirectOffsetOnAxis(smalli[0:SW, s:s + 1], 0)).then_inc(S["rows_in"], 16)
            pool.wait_ge(S["off_ready"], 1)
            pool.wait_ge(S["runs_out"], 16)
            for s in range(2):
                nc.gpsimd.indirect_dma_start(runb[0:SW, s, :], None, runs_d[:, :],
                                             bass.IndirectOffsetOnAxis(smalli[0:SW, 2 + s:3 + s], 0)).then_inc(S["runs_in"], 16)
            pool.wait_ge(S["ed_ready"], 1)
            with pool.Fori(0, 2) as s:
                with pool.Fori(0, SW // 4) as j:
                    for h in range(2):
                        pool.wait_ge(S["c_done"], s * (SW // 2) + j * 2 + (h + 1))
                        own = sls[:, bass.ds(s, 1), :, bass.ds(j * 4 + h * 2, 2)].rearrange("p s t w -> p (s t) w")
                        nc.gpsimd.tensor_copy(own6[h], own).then_inc(S["own_in"], 1)
                        pool.wait_ge(S["own_in"], s * (SW // 2) + j * 2 + (h + 1))
                        pool.sem_inc(S["own_seen"], 1)
                        for c in range(2):
                            for t in range(RUN):
                                last = nc.gpsimd.tensor_scalar(ohs[(h * 2 + c) * RUN + t], i_s[:, :], own6[h][:, t, c:c + 1],
                                                               None, ALU.is_equal)
                        last.then_inc(S["oh_s"], 1)

        @block.scalar
        def _(act):
            copy = ACT.Copy
            n = 0
            for kt in range(KT):
                for t0 in range(0, NT, 4):
                    w = min(4, NT - t0) * P
                    act.wait_ge(S["x_tr"], n + 1)
                    nc.scalar.activation(xT[:, kt, t0 * P:t0 * P + w], ps[n % 2][:, 0:w], copy).then_inc(S["xt_ready"], 1)
                    n += 1

            def logit_weights(lay):
                n0 = lay.n * R * KT

                def product(i):
                    act.wait_ge(S["wq_done"], n0 + i + 1)
                    r, kt = i // KT, i % KT
                    o = lay.wqk[:, kt, :].rearrange("p (a r h) -> p a r h", a=2, r=R)[:, :, r, :]
                    nc.scalar.activation(o, ps[4 + i % 2][:, 0:2 * lay.H].rearrange("p (a h) -> p a h", a=2), copy).then_inc(S["wq_ready"], 1)

                if lay is L2:
                    for i in range(2):
                        act.wait_ge(xr_out[i], 16 * RS // 2)
                for i in range(R * KT):
                    act.wait_ge(S["wt_tr"], n0 + i + 1)
                    if i >= 2:
                        act.wait_ge(S["wq_done"], n0 + i - 1)
                    for b in range(2):
                        last = nc.scalar.activation(WT[i % 2][:, b * HF:(b + 1) * HF], ps[2 * (i % 2) + b][:, 0:HF], copy)
                    last.then_inc(S["wt_ready"], 1)
                    if i >= 1:
                        product(i - 1)
                product(R * KT - 1)

            def logits(lay):
                act.wait_ge(S["qk_done"], lay.n + 1)
                v = ps[6][:, 0:NT * lay.C].rearrange("p (t c) -> p t c", t=NT)
                nc.scalar.activation(lay.qk[:, :, :], v, copy)
                nc.scalar.activation(lay.ks[:, :, :], v[:, :, lay.C // 2:], copy, scale=SLOPE).then_inc(S["qk_ready"], 1)

            logit_weights(L1)
            logits(L1)
            act.sem_inc(S["c_ready"], 2)
            with act.Fori(0, NW // 4) as j:
                for h in range(2):
                    act.wait_ge(S["c_done"], j * 2 + (h + 3))
                    for c in range(2):
                        last = nc.scalar.activation(Ct[:, :, bass.ds(j * (4 * WIN) + (2 * h + c) * WIN, WIN)],
                                                    ps[h][:, c * WM:(c + 1) * WM].rearrange("p (a b) -> p a b", b=WIN), copy)
                    last.then_inc(S["c_ready"], 1)

            def transform(lay):
                act.wait_ge(S["ones_in"], lay.n + 1)
                for n in range(RS):
                    act.wait_ge(S["t_done"], lay.n * RS + n + 1)
                    if n >= 2:
                        act.wait_ge(xr_out[n % 2], 16 * (lay.n * RS // 2 + n // 2))
                    for b in range(2):
                        bank = ps[2 * (n % 2) + b][:, 0:HF]
                        if lay is L1:
                            o = stg1[n % 2][:, b, :].rearrange("p (h c) -> p h c", h=2)[:, :, 0:HD]
                            last = nc.scalar.activation(o, bank.rearrange("p (h c) -> p h c", h=2), copy)
                        else:
                            last = nc.scalar.activation(stg[n % 2][:, b * (HF + 1):b * (HF + 1) + HF], bank, copy)
                    last.then_inc(S["t_evac"], 1)

            def ab_rows(lay):
                act.wait_ge(S["ab_tr"], lay.n + 1)
                for b in range(3):
                    w = min(512, NP - 512 * b)
                    last = nc.scalar.activation(rows[0:lay.C, b * 512:b * 512 + w], ps[b][0:lay.C, 0:w], copy)
                last.then_inc(S["ab_rows"], 1)

            transform(L1)
            logit_weights(L2)
            ab_rows(L1)

            def ht_out(g):
                hp, dh = group1(g)
                for c in range(3):
                    act.wait_ge(S["h_tr"], 3 * g + c + 1)
                    nc.scalar.activation(xT[:, hp * 3 + c, dh * DH:dh * DH + 512], ps[5][:, :], copy)
                    nc.scalar.activation(xT[:, hp * 3 + c, dh * DH + 512:(dh + 1) * DH], ps[6][:, 0:DH - 512], copy).then_inc(S["ht_ready"], 1)

            for g in range(NG1):
                hp, dh = group1(g)
                for r in range(R):
                    act.wait_ge(ab_in[r], 16 * (g + 1))
                with act.Fori(0, R) as r:
                    for t in range(NT):
                        step = r * NT + (g * RS + t)
                        act.wait_ge(S["a_used"], step + 1)
                        act.wait_ge(S["e2_free"], step + 1)
                        for h in range(2):
                            col = r * H + (hp * 2 + h)
                            nc.scalar.activation(e1[t % 5][:, h, :], abr[:, bass.ds(r, 1), h, :].rearrange("p a d -> p (a d)"), ACT.Exp,
                                                 bias=qk1t[:, t, bass.ds(col + R * H, 1)])
                            last = nc.scalar.activation(e2[t % 2][:, h, :], abr[:, bass.ds(r, 1), 2 + h, :].rearrange("p a d -> p (a d)"), ACT.Exp,
                                                        bias=ks1[:, t, bass.ds(col, 1)])
                        last.then_inc(S["e_ready"], 1)
                if g:
                    ht_out(g - 1)
                act.wait_ge(S["h_lin"], g + 1)
                nc.scalar.activation(hmn, hmn, ACT.Exp).then_inc(S["h_exp"], 1)
            ht_out(NG1 - 1)
            logits(L2)
            transform(L2)
            ab_rows(L2)
            for g, (t0, t1) in enumerate(GROUPS):
                w = (t1 - t0) * P
                for r in range(R):
                    act.wait_ge(ab_in[r], 16 * (NG1 + g + 1))
                with act.Fori(0, R) as r:
                    for t in range(NT):
                        step = r * NT + (NST + g * RS + t)
                        act.wait_ge(S["a_used"], step + 1)
                        act.wait_ge(S["e2_free"], step + 1)
                        nc.scalar.activation(g1[t % 5][:, 0:w], ab2r[:, bass.ds(r, 1), 0, 0:w].rearrange("p a d -> p (a d)"), ACT.Exp,
                                             bias=qk2t[:, t, bass.ds(r + R, 1)])
                        nc.scalar.activation(g2[t % 2][:, 0:w], ab2r[:, bass.ds(r, 1), 1, 0:w].rearrange("p a d -> p (a d)"), ACT.Exp,
                                             bias=ks2[:, t, bass.ds(r, 1)]).then_inc(S["e_ready"], 1)
                act.wait_ge(S["o_var"], g + 1)
                m = t1 - t0
                nc.scalar.activation(mv[:, 0:m, 1], mv[:, 0:m, 1], ACT.Sqrt).then_inc(S["o_std"], 1)

        @block.tensor
        def _(pe):
            mm = nc.tensor.matmul
            pe.wait_ge(S["consts"], 8)
            pe.wait_ge(S["ranks"], 1)
            for s in range(2):
                last = mm(ps[7][0:SW, s:s + 1], G[0:EP, s * SW:(s + 1) * SW], onesf[0:EP, 0:1], start=True, stop=True)
            last.then_inc(S["ranks"], 1)
            pe.wait_ge(S["x_in"], 32)
            n = 0
            for kt in range(KT):
                for t0 in range(0, NT, 4):
                    if n >= 2:
                        pe.wait_ge(S["xt_ready"], n - 1)
                    for t in range(t0, min(t0 + 4, NT)):
                        last = nc.tensor.transpose(ps[n % 2][:, (t - t0) * P:(t - t0 + 1) * P], x_sb[:, t, kt * P:(kt + 1) * P], ident[:, :])
                    last.then_inc(S["x_tr"], 1)
                    n += 1

            def logit_weights(lay):
                n0 = lay.n * R * KT
                pe.wait_ge(S["qv_in"], 64)

                def transposes(i):
                    r, kt = i // KT, i % KT
                    n = WOFF[2 * lay.n] + r
                    if kt == 0:
                        pe.wait_ge(w_in[n % 2], 16 * (n // 2 + 1))
                    if i >= 2:
                        pe.wait_ge(S["wt_ready"], n0 + i - 1)
                    elif lay is L1:
                        pe.wait_ge(S["xt_ready"], NB_X)
                    else:
                        pe.wait_ge(S["t_evac"], RS)
                    for ft in range(KT):
                        last = nc.tensor.transpose(ps[2 * (i % 2) + ft // 3][:, (ft % 3) * P:(ft % 3 + 1) * P],
                                                   wslot[n % 2][:, kt, ft * P:(ft + 1) * P], ident[:, :])
                    last.then_inc(S["wt_tr"], 1)

                def product(i):
                    r, kt = i // KT, i % KT
                    n = WOFF[2 * lay.n] + r
                    pe.wait_ge(S["wt_ready"], n0 + i + 1)
                    if i >= 2:
                        pe.wait_ge(S["wq_ready"], n0 + i - 1)
                    for ft in range(KT):
                        last = mm(ps[4 + i % 2][:, 0:2 * lay.H], WT[i % 2][:, ft * P:(ft + 1) * P], lay.qv[:, ft, :],
                                  start=ft == 0, stop=ft == KT - 1)
                    last.then_inc(S["wq_done"], 1)

                transposes(0)
                for i in range(R * KT):
                    if i + 1 < R * KT:
                        transposes(i + 1)
                    product(i)

            def logits(lay):
                pe.wait_ge(S["wq_ready"], (lay.n + 1) * R * KT)
                for t in range(NT):
                    for kt in range(KT):
                        last = mm(ps[6][:, t * lay.C:(t + 1) * lay.C], xT[:, kt, t * P:(t + 1) * P], lay.wqk[:, kt, :],
                                  start=kt == 0, stop=kt == KT - 1)
                last.then_inc(S["qk_done"], 1)

            logit_weights(L1)
            logits(L1)
            pe.wait_ge(S["runs_in"], 32)
            for s in range(2):
                for t in range(RUN):
                    c = (s * RUN + t) * SW
                    last = nc.tensor.transpose(ps[7][:, c:c + SW], runb[0:SW, s, t * P:(t + 1) * P], ident[0:SW, 0:SW])
            last.then_inc(S["run_tr"], 1)
            pe.wait_ge(S["flag_sum"], 1)
            pe.wait_ge(S["qk_ready"], 1)
            mm(ps[6][0:1, 0:1], small[:, 8:9], onesf[:, 0:1], start=True, stop=True).then_inc(S["flag_tot"], 1)
            pe.sem_inc(S["c_done"], 2)
            pe.wait_ge(S["wt_ready"], R * KT)
            with pe.Fori(0, NW // 4) as j:
                for h in range(2):
                    pe.wait_ge(S["oh_s"], j * 2 + (h + 1))
                    pe.wait_ge(S["oh_m"], j * 2 + (h + 1))
                    pe.wait_ge(S["c_ready"], j * 2 + (h + 1))
                    for c in range(2):
                        for t in range(RUN):
                            n = (h * 2 + c) * RUN + t
                            last = mm(ps[h][:, c * WM:(c + 1) * WM], ohs[n], ohm[n], start=t == 0, stop=t == RUN - 1)
                    last.then_inc(S["c_done"], 1)
            pe.wait_ge(S["flag_ready"], 1)
            held = pe.value_load(smalli[0:1, 4:5], min_val=0, max_val=E)
            with pe.If(held < E):
                pe.wait_ge(S["c_ready"], NW // 2 + 2)
                with pe.Fori(0, NW) as w:
                    pe.wait_ge(S["fb_free"], w + 1)
                    mm(ps[0][:, 0:WM], zm[:, 0:P], zm[:, 0:WM], start=True, stop=False, skip_group_check=True)
                    with pe.Fori(0, EC // 4) as j:
                        pe.wait_ge(S["fb_built"], w * (EC // 4) + j + 1)
                        for t in range(4):
                            last = mm(ps[0][:, 0:WM], ohs[t][0:EP, :], ohm[t][0:EP, :], start=False, stop=True, skip_group_check=True)
                        last.then_inc(S["fb_used"], 1)
                    last = mm(ps[0][:, 0:WM], zm[:, 0:P], zm[:, 0:WM], start=False, stop=True, skip_group_check=True)
                    last.then_inc(S["fb_done"], 1)
                pe.wait_ge(S["fb_evac"], NW)

            def transform(lay, r):
                n = WOFF[2 * lay.n + 1] + r
                pe.wait_ge(w_in[n % 2], 16 * (n // 2 + 1))
                for t in range(NT):
                    i = lay.n * RS + r * NT + t
                    if r * NT + t >= 2:
                        pe.wait_ge(S["t_evac"], i - 1)
                    elif lay is L1:
                        pe.wait_ge(S["c_ready"], NW // 2 + 2)
                    for kt in range(KT):
                        for b in range(2):
                            last = mm(ps[2 * (t % 2) + b][:, 0:HF], xT[:, kt, t * P:(t + 1) * P],
                                      wslot[n % 2][:, kt, b * HF:(b + 1) * HF], start=kt == 0, stop=kt == KT - 1)
                    last.then_inc(S["t_done"], 1)

            def mk_transposes(lay, u):
                u0 = u if lay is L1 else R
                pe.wait_ge(S["mk_step"], (u + 1) * NT * H if lay is L1 else RS * (H + 1))
                for t in range(NT):
                    i = u0 * NT + t
                    if i >= 2:
                        pe.wait_ge(S["mk_red"], i - 1)
                    for c in range(len(lay.units[u])):
                        last = nc.tensor.transpose(ps[6 + i % 2][:, c * P:(c + 1) * P], Mk[u0 % 2][:, c, t * P:(t + 1) * P], ident[:, :])
                    last.then_inc(S["mk_tr"], 1)

            def ab_transposes(lay):
                pe.wait_ge(S["ab_ready"], lay.n + 1)
                pe.wait_ge(S["t_evac"], (lay.n + 1) * RS)
                pe.wait_ge(S["wt_ready"], 2 * R * KT)
                for t in range(NT):
                    last = nc.tensor.transpose(ps[t // 4][0:lay.C, (t % 4) * P:(t % 4 + 1) * P], lay.ab[:, t, :], ident[:, :])
                last.then_inc(S["ab_tr"], 1)

            transform(L1, 0)
            transform(L1, 1)
            mk_transposes(L1, 0)
            transform(L1, 2)
            mk_transposes(L1, 1)
            logit_weights(L2)
            mk_transposes(L1, 2)
            ab_transposes(L1)

            def h_transposes(g):
                pe.wait_ge(S["h_ready"], g + 1)
                for c in range(3):
                    if 3 * g + c:
                        pe.wait_ge(S["ht_ready"], 3 * g + c)
                    for t in range(DT):
                        last = nc.tensor.transpose(ps[5 + t // 4][:, (t % 4) * P:(t % 4 + 1) * P], hst[:, t, c * P:(c + 1) * P], ident[:, :])
                    last.then_inc(S["h_tr"], 1)

            pe.sem_inc(S["a_used"], RING)
            pe.wait_ge(S["ab_rows"], 1)
            for g in range(NG1):
                if g:
                    pe.wait_ge(S["g_free"], g)
                for i in range(DT):
                    mm(ps[i][:, 0:XB], zm[:, 0:P], zm[:, 0:XB], start=True, stop=False, skip_group_check=True)
                with pe.Fori(0, R) as r:
                    for t in range(NT):
                        step = r * NT + (g * RS + t)
                        pe.wait_ge(S["a_ready"], step + 1)
                        pe.wait_ge(xr_in[t % NX], r * (16 * NT // NX) + 16 * (g * RS // NX + t // NX + 1))
                        for h in range(2):
                            for i in range(DT):
                                o = h * (HD + 1)
                                last = mm(ps[i][:, o:o + HD + 1], e1[t % 5][:, h, i * P:(i + 1) * P], xring[t % NX][:, o:o + HD + 1],
                                          start=False, stop=True, skip_group_check=True)
                        last.then_inc(S["a_used"], 1)
                if g:
                    h_transposes(g - 1)
            h_transposes(NG1 - 1)

            pe.wait_ge(S["ht_ready"], 3 * NG1)
            logits(L2)
            transform(L2, 0)
            transform(L2, 1)
            mk_transposes(L2, 0)
            transform(L2, 2)
            ab_transposes(L2)
            pe.wait_ge(S["ab_rows"], 2)
            for g, (t0, t1) in enumerate(GROUPS):
                if g:
                    pe.wait_ge(S["g_free"], NG1 + g)
                for i in range(t1 - t0):
                    for b in range(2):
                        mm(ps[2 * i + b][:, 0:HF + 1], zm[:, 0:P], zm[:, 0:HF + 1], start=True, stop=False, skip_group_check=True)
                with pe.Fori(0, R) as r:
                    for t in range(NT):
                        step = r * NT + (NST + g * RS + t)
                        pe.wait_ge(S["a_ready"], step + 1)
                        pe.wait_ge(xr_in[t % NX], r * (16 * NT // NX) + 16 * ((NST + g * RS) // NX + t // NX + 1))
                        for i in range(t1 - t0):
                            a = g1[t % 5][:, i * P:(i + 1) * P]
                            mm(ps[2 * i][:, 0:HF + 1], a, x2ring[t % NX][:, 0:HF + 1], start=False, stop=True, skip_group_check=True)
                            last = mm(ps[2 * i + 1][:, 0:HF], a, x2ring[t % NX][:, HF + 1:XW], start=False, stop=True, skip_group_check=True)
                        last.then_inc(S["a_used"], 1)

        @block.vector
        def _(dve):
            V = nc.vector
            links = [0]

            def link(ins):
                links[0] += 1
                ins.then_inc(S["chain"], 1)
                dve.wait_ge(S["chain"], links[0])

            V.memset(x_sb[:, NT - 1, :], 0.0).then_inc(S["x_zero"], 1)
            V.memset(f1[0:1, 0:PADL], float(2047 * CODE_DST)).then_inc(S["chain"], 1)
            links[0] += 1
            dve.wait_ge(S["edges_in"], 48)
            link(V.scalar_tensor_tensor(tmpf[0:EP, :], eti[0:EP, :], float(CODE_TYPE), srci[0:EP, :], ALU.mult, ALU.add))
            link(V.scalar_tensor_tensor(code[0:EP, :], dsti[0:EP, :], float(CODE_DST), tmpf[0:EP, :], ALU.mult, ALU.add))
            dve.sem_inc(S["code_ready"], 1)
            dve.wait_ge(S["consts"], 8)
            link(V.tensor_scalar(wrow, wrow, float(WIN * CODE_DST), None, ALU.mult))
            link(V.tensor_scalar(small[:, 2:4], small[:, 0:2], float(WIN * CODE_DST), None, ALU.mult))
            V.tensor_scalar(G[0:EP, :], wrow[0:EP, :], code[0:EP, 0:1], None, ALU.is_gt).then_inc(S["ranks"], 1)
            dve.wait_ge(S["ranks"], 2)
            link(V.tensor_scalar(small[0:SW, 4:6], ps[7][0:SW, 0:2], -1.0, 0.0, ALU.add, ALU.max))
            V.tensor_copy(smalli[0:SW, 0:2], small[0:SW, 4:6]).then_inc(S["row_ready"], 1)
            dve.wait_ge(S["rows_in"], 32)
            for s in range(2):
                link(V.tensor_scalar(tmpf[0:SW, :], rowb[0:SW, s, :], small[0:SW, 2 + s:3 + s], 0.0, ALU.is_lt, ALU.add,
                                     accum_out=small[0:SW, 6 + s:7 + s]))
            link(V.scalar_tensor_tensor(small[0:SW, 10:12], small[0:SW, 4:6], float(EC), small[0:SW, 6:8], ALU.mult, ALU.add))
            link(V.tensor_scalar(small[0:SW, 10:12], small[0:SW, 10:12], float(E - 1), None, ALU.min))
            link(V.tensor_copy(smalli[0:SW, 2:4], small[0:SW, 10:12]))
            V.tensor_scalar(smalli[0:SW, 2:4], smalli[0:SW, 2:4], GRAN.bit_length() - 1, None, ALU.logical_shift_right).then_inc(S["off_ready"], 1)

            def unpack(codes, p, n, dsth, dstl, rs, t0, t1, slo_o):
                link(V.tensor_scalar(t0, codes, P - 1, None, ALU.bitwise_and))
                link(V.tensor_copy(slo_o, t0))
                link(V.tensor_scalar(t0, codes, 7, 63, ALU.logical_shift_right, ALU.bitwise_and))
                link(V.tensor_scalar(t1, codes, 11, 3, ALU.logical_shift_right, ALU.bitwise_and))
                link(V.scalar_tensor_tensor(rs, t1, float(NT - 16), t0, ALU.mult, ALU.add))
                link(V.tensor_scalar(t0, codes, 13, WIN - 1, ALU.logical_shift_right, ALU.bitwise_and))
                link(V.scalar_tensor_tensor(rs, rs, float(WIN), t0, ALU.mult, ALU.add))
                link(V.tensor_scalar(t0, codes, 16, None, ALU.logical_shift_right))
                link(V.tensor_copy(dsth, t0))

            dve.wait_ge(S["run_tr"], 1)
            link(V.tensor_copy(edi, ps[7][:, 0:NE]))
            unpack(edi, P, NE, f0, None, f1, u0, u1, slo)
            link(V.tensor_tensor(f0, f0, wid, ALU.is_equal))
            link(V.scalar_tensor_tensor(mcode, f1, 1.0, f0, ALU.add, ALU.mult))
            link(V.tensor_scalar(mcode, mcode, -1.0, None, ALU.add))
            dve.sem_inc(S["ed_ready"], 1)
            V.reduce_sum(small[:, 8:9], f0, AX).then_inc(S["flag_sum"], 1)
            with dve.Fori(0, 2) as s:
                with dve.Fori(0, SW // 4) as j:
                    for h in range(2):
                        dve.wait_ge(S["c_done"], s * (SW // 2) + j * 2 + (h + 1))
                        for c in range(2):
                            for t in range(RUN):
                                last = V.tensor_scalar(ohm[(h * 2 + c) * RUN + t], i_m[:, :],
                                                       mcode[:, bass.ds(s * (RUN * SW) + j * 4 + (t * SW + h * 2 + c), 1)],
                                                       None, ALU.is_equal)
                        last.then_inc(S["oh_m"], 1)
            dve.wait_ge(S["flag_tot"], 1)
            V.tensor_copy(smalli[0:1, 4:5], ps[6][0:1, 0:1]).then_inc(S["flag_ready"], 1)
            dve.wait_ge(S["c_ready"], NW // 2 + 2)
            dve.wait_ge(S["flag_ready"], 1)
            held = dve.value_load(smalli[0:1, 4:5], min_val=0, max_val=E)
            with dve.If(held < E):
                before = links[0]
                nat = edi[0:EP, 0:EC]
                link(V.tensor_copy(nat, code[0:EP, :]))
                unpack(nat, EP, EC, f0[0:EP, 0:EC], None, f1[0:EP, 0:EC], u0[0:EP, 0:EC], u1[0:EP, 0:EC], slo[0:EP, 0:EC])
                dve.sem_inc(S["fb_used"], 1)
                with dve.Fori(0, NW) as w:
                    dve.sem_inc(S["fb_free"], 1)
                    V.tensor_scalar(wid[0:EP, 0:EC], f0[0:EP, 0:EC], float(WIN * CODE_DST), wrow[0:EP, bass.ds(w, 1)], ALU.mult, ALU.is_equal).then_inc(S["fb_c"], 1)
                    dve.wait_ge(S["fb_c"], w * 2 + 1)
                    V.scalar_tensor_tensor(mcode[0:EP, 0:EC], f1[0:EP, 0:EC], 1.0, wid[0:EP, 0:EC], ALU.add, ALU.mult).then_inc(S["fb_c"], 1)
                    with dve.Fori(0, EC // 4) as j:
                        dve.wait_ge(S["fb_c"], w * 2 + 2)
                        dve.wait_ge(S["fb_used"], w * (EC // 4) + j + 1)
                        for t in range(4):
                            V.tensor_scalar(ohs[t][0:EP, :], i_s[0:EP, :], slo[0:EP, bass.ds(j * 4 + t, 1)], None, ALU.is_equal)
                            last = V.tensor_scalar(ohm[t][0:EP, :], i_m[0:EP, :], 1.0, mcode[0:EP, bass.ds(j * 4 + t, 1)], ALU.add, ALU.is_equal)
                        last.then_inc(S["fb_built"], 1)
                    dve.wait_ge(S["fb_done"], w + 1)
                    V.tensor_copy(Ct[:, :, bass.ds(w * WIN, WIN)], ps[0][:, 0:WM].rearrange("p (a b) -> p a b", b=WIN)).then_inc(S["fb_evac"], 1)
                    dve.wait_ge(S["fb_evac"], w + 1)
                fb_links = links[0] - before
            with dve.Else():
                dve.sem_inc(S["chain"], fb_links)

            def ones(lay):
                for s in range(2):
                    if lay is L1:
                        last = V.memset(stg1[s].rearrange("p a (h c) -> p a h c", h=2)[:, :, :, HD], 1.0)
                    else:
                        last = V.memset(stg[s][:, HF:HF + 1], 1.0)
                last.then_inc(S["ones_in"], 1)

            steps = [0, 0]

            def maxima(lay, u):
                u0 = u if lay is L1 else R
                cols = lay.units[u]
                m = Mk[u0 % 2]
                started = {}
                for r in sorted({r for r, _ in cols}):
                    for t in range(NT):
                        i = steps[1]
                        if i >= 2:
                            dve.wait_ge(S["mk_step"], started_at[i - 2])
                        V.tensor_scalar(cneg[i % 2], Ct[:, r * NT + t, :], 0.0, -BIG, ALU.is_equal, ALU.mult).then_inc(S["mk_cneg"], 1)
                        dve.wait_ge(S["mk_cneg"], i + 1)
                        steps[1] += 1
                        for c, (rr, h) in enumerate(cols):
                            if rr != r:
                                continue
                            k = lay.qk[:, t, R * lay.H + r * lay.H + h:R * lay.H + r * lay.H + h + 1]
                            if t == 0:
                                last = V.tensor_scalar(m[:, c, :], cneg[i % 2], k, None, ALU.add)
                            else:
                                dve.wait_ge(S["mk_step"], started[c])
                                last = V.scalar_tensor_tensor(m[:, c, :], cneg[i % 2], k, m[:, c, :], ALU.add, ALU.max)
                            steps[0] += 1
                            started[c] = steps[0]
                            last.then_inc(S["mk_step"], 1)
                        started_at.append(steps[0])

            started_at = []

            def reduce(lay, u):
                u0 = u if lay is L1 else R
                n = len(lay.units[u])
                for t in range(NT):
                    i = u0 * NT + t
                    dve.wait_ge(S["mk_tr"], i + 1)
                    o = lay.mk[:, t, u, :] if lay is L1 else lay.mk[:, t, :, 0]
                    V.reduce_max(o, ps[6 + i % 2][:, 0:n * P].rearrange("p (c s) -> p c s", c=n), AX).then_inc(S["mk_red"], 1)

            def shifts(lay):
                dve.wait_ge(S["mk_red"], (R if lay is L1 else R + 1) * NT)
                H_ = lay.H
                q = lay.qk[:, :, 0:R * H_].rearrange("p t (r h) -> p t r h", r=R)
                k = lay.mk
                m, n, o = lay.mx[:, 0], lay.mx[:, 1], lay.mx[:, 2]
                link(V.tensor_tensor(m, q[:, :, 0, :], k[:, :, 0, :], ALU.add))
                for r in range(1, R):
                    link(V.tensor_tensor(n, q[:, :, r, :], k[:, :, r, :], ALU.add))
                    link(V.tensor_tensor(m, m, n, ALU.max))
                link(V.tensor_scalar(n, m, -BIG / 2, None, ALU.is_gt))
                link(V.scalar_tensor_tensor(o, m, SLOPE, m, ALU.mult, ALU.max))
                link(V.tensor_tensor(m, o, n, ALU.mult))
                w = min(2, H_)
                for r in range(R):
                    for hp in range(H_ // w):
                        c = (r * (H_ // w) + hp) * 2 * w
                        qq, mm_ = q[:, :, r, hp * w:(hp + 1) * w], m[:, :, hp * w:(hp + 1) * w]
                        V.tensor_tensor(lay.ab[:, :, c:c + w], qq, mm_, ALU.subtract)
                        last = V.scalar_tensor_tensor(lay.ab[:, :, c + w:c + 2 * w], qq, SLOPE, mm_, ALU.mult, ALU.subtract)
                last.then_inc(S["ab_ready"], 1)

            dve.wait_ge(S["oh_s"], NW // 2)
            ones(L1)
            dve.wait_ge(S["qk_ready"], 1)
            maxima(L1, 0)
            maxima(L1, 1)
            reduce(L1, 0)
            maxima(L1, 2)
            reduce(L1, 1)
            reduce(L1, 2)
            shifts(L1)

            dve.sem_inc(S["e2_free"], 2)
            dve.wait_ge(S["bias_in"], 32)
            for g in range(NG1):
                hp, dh = group1(g)
                with dve.Fori(0, R) as r:
                    for t in range(NT):
                        step = r * NT + (g * RS + t)
                        dve.wait_ge(S["e_ready"], step + 1)
                        V.tensor_tensor(e1[t % 5], e1[t % 5], e2[t % 2], ALU.max).then_inc(S["e2_free"], 1)
                        dve.wait_ge(S["e2_free"], step + 3)
                        cc = Ct[:, bass.ds(r * NT + t, 1), dh * DH:(dh + 1) * DH].broadcast_to([P, 2, DH])
                        V.scalar_tensor_tensor(e1[t % 5], e1[t % 5], 1.0, cc, ALU.min, ALU.mult).then_inc(S["a_ready"], 1)
                dve.wait_ge(S["a_used"], RING + (g + 1) * RS)
                if g:
                    dve.wait_ge(S["h_tr"], 3 * g)
                z = small[:, 16:16 + 2 * DT].rearrange("p (t h) -> p t h", h=2)
                for i in range(DT):
                    V.tensor_scalar(z[:, i, :], ps[i][:, 0:XB].rearrange("p (h c) -> p h c", h=2)[:, :, HD], Z_EPS, None, ALU.add)
                link(V.memset(small[:, 40:41], 0.0))
                link(V.reciprocal(z, z))
                for i in range(DT):
                    for h in range(2):
                        o = h * (HD + 1)
                        last = V.scalar_tensor_tensor(hst[:, i, h * HD:(h + 1) * HD], ps[i][:, o:o + HD], z[:, i, h:h + 1],
                                                      b1b[:, hp * HF + h * HD:hp * HF + (h + 1) * HD], ALU.mult, ALU.add)
                last.then_inc(S["g_free"], 1)
                dve.wait_ge(S["g_free"], g + 1)
                V.tensor_scalar(hmn, hst, 0.0, None, ALU.min).then_inc(S["h_lin"], 1)
                link(V.tensor_scalar(hst, hst, 0.0, None, ALU.max))
                dve.wait_ge(S["h_exp"], g + 1)
                V.scalar_tensor_tensor(hst, hmn, -1.0, hst, ALU.add, ALU.add).then_inc(S["h_ready"], 1)

            dve.wait_ge(S["h_tr"], 3 * NG1)
            ones(L2)
            dve.wait_ge(S["qk_ready"], 2)
            maxima(L2, 0)
            reduce(L2, 0)
            shifts(L2)
            for g, (t0, t1) in enumerate(GROUPS):
                w = (t1 - t0) * P
                m = t1 - t0
                with dve.Fori(0, R) as r:
                    for t in range(NT):
                        step = r * NT + (NST + g * RS + t)
                        dve.wait_ge(S["e_ready"], step + 1)
                        V.tensor_tensor(g1[t % 5][:, 0:w], g1[t % 5][:, 0:w], g2[t % 2][:, 0:w], ALU.max).then_inc(S["e2_free"], 1)
                        dve.wait_ge(S["e2_free"], step + 3)
                        cc = Ct[:, bass.ds(r * NT + t, 1), t0 * P:t1 * P].rearrange("p a d -> p (a d)")
                        V.scalar_tensor_tensor(g1[t % 5][:, 0:w], g1[t % 5][:, 0:w], 1.0, cc, ALU.min, ALU.mult).then_inc(S["a_ready"], 1)
                dve.wait_ge(S["a_used"], RING + NST + (g + 1) * RS)
                if g:
                    dve.wait_ge(S["o_out"], 16 * t0)
                z = small[:, 16:16 + GT]
                for i in range(m):
                    V.tensor_scalar(z[:, i:i + 1], ps[2 * i][:, HF:HF + 1], Z_EPS, None, ALU.add)
                link(V.memset(small[:, 40:41], 0.0))
                link(V.reciprocal(z[:, 0:m], z[:, 0:m]))
                for i in range(m):
                    for b in range(2):
                        last = V.scalar_tensor_tensor(ost[:, i, b * HF:(b + 1) * HF], ps[2 * i + b][:, 0:HF], z[:, i:i + 1],
                                                      b2b[:, b * HF:(b + 1) * HF], ALU.mult, ALU.add)
                last.then_inc(S["g_free"], 1)
                dve.wait_ge(S["g_free"], NG1 + g + 1)
                dve.wait_ge(xres_in, 16 * t1)
                for i in range(m):
                    k = TAIL if t0 + i == NT - 1 else P
                    last = V.tensor_tensor(ost[0:k, i, :], ost[0:k, i, :], xres[0:k, i, :], ALU.add)
                link(last)
                for i in range(m):
                    for b in range(2):
                        last = V.bn_stats(st6[:, i, b * 6:(b + 1) * 6], ost[:, i, b * HF:(b + 1) * HF])
                link(last)
                for i in range(m):
                    last = V.bn_aggr(mv[:, i, :], st6[:, i, :])
                link(last)
                V.tensor_scalar(mv[:, 0:m, 1], mv[:, 0:m, 1], LN_EPS, None, ALU.add).then_inc(S["o_var"], 1)
                dve.wait_ge(S["o_std"], g + 1)
                link(V.reciprocal(mv[:, 0:m, 1], mv[:, 0:m, 1]))
                for i in range(m):
                    V.tensor_scalar(ost[:, i, :], ost[:, i, :], mv[:, i, 0:1], mv[:, i, 1:2], ALU.subtract, ALU.mult).then_inc(S["o_ready"], 1)


_INS = ["x", "src", "dst", "edge_type_3", "L0_gnn_W1", "L0_gnn_q1", "L0_gnn_k1", "L0_gnn_b1",
        "L0_gnn_W2", "L0_gnn_q2", "L0_gnn_k2", "L0_gnn_b2"]


def kernel(**inputs):
    import numpy as _np
    import concourse.bacc as _bacc
    from concourse import mybir as _mybir
    from concourse.bass_utils import run_bass_kernel_spmd as _run

    nc = _bacc.Bacc("TRN2", target_bir_lowering=False, num_devices=1)
    arrays, args = {}, []
    for name in _INS:
        a = _np.ascontiguousarray(inputs[name])
        arrays[f"in_{name}"] = a
        args.append(nc.dram_tensor(f"in_{name}", a.shape, _mybir.dt.from_np(a.dtype), kind="ExternalInput").ap())
    out = nc.dram_tensor("out", inputs["x"].shape, _mybir.dt.float32, kind="ExternalOutput").ap()
    rgat(nc, *args, out)
    r = _run(nc, [arrays], core_ids=[0])
    return r.results[0]["out"]
```

```python
from contextlib import ExitStack

import concourse.bass as bass
from concourse import mybir

P = 128
F32 = mybir.dt.float32
BF16 = mybir.dt.bfloat16
I32 = mybir.dt.int32
U32 = mybir.dt.uint32
U16 = mybir.dt.uint16
ALU = mybir.AluOpType
ACT = mybir.ActivationFunctionType
AX = mybir.AxisListType.X

SLOPE = 0.2
Z_EPS = 1e-16
LN_EPS = 1e-5
BIG = 1e30
CODE_DST = 8192
CODE_TYPE = 2048
WIN = 8
RUN = 3
GRAN = 32


def rgat(nc, x, src, dst, etype, W1, q1, k1, b1, W2, q2, k2, b2, out):
    N, F = x.shape
    E = src.shape[0]
    R = W1.shape[0]
    H = q1.shape[1]
    HD = F // H
    KT = F // P
    NT = (N + P - 1) // P
    NP = NT * P
    TAIL = N - (NT - 1) * P
    RS = R * NT
    HP = H // 2
    QC = 2 * R * H
    QC2 = 2 * R
    HF = F // 2
    EP = 125
    EC = E // EP
    NW = NP // WIN
    SW = NW // 2
    WM = RS * WIN
    RUNL = RUN * P
    NROW = E // GRAN
    PADL = RUNL
    XB = 2 * (HD + 1)
    DH = NP // 2
    DT = NT // 2
    XW = F + 1
    assert EP * EC == E and R == 3 and H == 4 and WM * 2 <= 512 and NW <= 2 * P and HD * 2 == HF

    code_d = nc.dram_tensor("code_d", [E + PADL], F32).ap()
    runs_d = nc.dram_tensor("runs_d", [NROW, RUNL], F32).ap()
    xr_d = nc.dram_tensor("xr_d", [RS, 2, P, XB], F32).ap()
    xr2_d = nc.dram_tensor("xr2_d", [RS, P, XW], F32).ap()
    ab_d = nc.dram_tensor("ab_d", [QC, NP], F32).ap()
    ab2_d = nc.dram_tensor("ab2_d", [QC2, NP], F32).ap()

    with ExitStack() as ctx:
        def sb(name, shape, dt=F32):
            return ctx.enter_context(nc.sbuf_tensor(name, shape, dt))

        def sem(name):
            return ctx.enter_context(nc.semaphore(name))

        Ct = sb("Ct", [P, RS, NP], U16)
        xT = sb("xT", [P, KT, NP])
        ident = sb("ident", [P, P])
        onesf = sb("onesf", [P, 2])
        zm = sb("zm", [P, 512], BF16)
        i_m = sb("i_m", [P, WM], BF16)
        i_s = sb("i_s", [P, P], BF16)
        qv1 = sb("qv1", [P, KT, 2 * H])
        qv2 = sb("qv2", [P, KT, 2])
        wqk1 = sb("wqk1", [P, KT, QC])
        wqk2 = sb("wqk2", [P, KT, QC2])
        qk1t = sb("qk1t", [P, NT, QC])
        ks1 = sb("ks1", [P, NT, R * H])
        qk2t = sb("qk2t", [P, NT, QC2])
        ks2 = sb("ks2", [P, NT, R])
        mk1 = sb("mk1", [P, NT, R, H])
        mk2 = sb("mk2", [P, NT, R, 1])
        mx1 = sb("mx1", [P, 4, NT, H])
        mx2 = sb("mx2", [P, 4, NT, 1])
        ab1 = sb("ab1", [P, NT, QC])
        ab2 = sb("ab2", [P, NT, QC2])
        b1b = sb("b1b", [P, F])
        b2b = sb("b2b", [P, F])
        code = sb("code", [P, EC])
        small = sb("small", [P, 64])
        smalli = sb("smalli", [P, 8], U32)
        ARENA = 22432
        ar = sb("arena", [P, ARENA])
        ps = [ctx.enter_context(nc.psum_tensor(f"ps{i}", [P, 512], F32)) for i in range(8)]

        def cut(at, n):
            assert at + n <= ARENA, (at, n)
            return ar[:, at:at + n]

        WS = KT * F
        wslot = [cut(i * WS, WS).rearrange("p (k f) -> p k f", k=KT) for i in range(2)]
        pos = [2 * WS]

        def take(n):
            pos[0] += n
            return cut(pos[0] - n, n)

        dsti, srci, eti = (take(EC).bitcast(I32) for _ in range(3))
        tmpf = take(EC)
        rowb = take(2 * EC).rearrange("p (s c) -> p s c", s=2)
        runb = take(2 * RUNL).rearrange("p (s c) -> p s c", s=2)
        NE = 2 * RUN * SW
        edi = take(NE).bitcast(I32)
        u0, u1 = take(NE).bitcast(I32), take(NE).bitcast(I32)
        f0, f1 = take(NE), take(NE)
        wid = take(NE)
        wrow = take(NW)
        G = take(NW)
        slo = take(NE)
        mcode = take(NE)
        NOH = 4 * RUN
        oh_s = take(NOH * P // 2).bitcast(BF16).rearrange("p (n s) -> p n s", n=NOH)
        ohs = [oh_s[:, i, :] for i in range(NOH)]
        ohm = [take(WM // 2).bitcast(BF16) for _ in range(NOH)]
        x_sb = Ct[:, :, :].rearrange("p a b -> p (a b)")[:, 0:2 * NT * F].bitcast(F32).rearrange("p (t f) -> p t f", t=NT)
        pos[0] = 2 * WS
        Mk = [take(H * NP).rearrange("p (h d) -> p h d", h=H) for _ in range(2)]
        cneg = [take(NP // 2).bitcast(BF16) for _ in range(2)]
        stg = [take(2 * XB) for _ in range(2)]
        WT = [s[:, 0:F] for s in stg]
        stg1 = [s.rearrange("p (a c) -> p a c", a=2) for s in stg]
        rows = Mk[0][:, 0, :]
        pos[0] = 0
        NX = 5
        abr = take(R * 4 * DH).rearrange("p (r c d) -> p r c d", r=R, c=4)
        e1 = [take(2 * DH).rearrange("p (h d) -> p h d", h=2) for _ in range(5)]
        e2 = [take(2 * DH).rearrange("p (h d) -> p h d", h=2) for _ in range(2)]
        xring = [take(XB) for _ in range(NX)]
        hst = take(DT * HF).rearrange("p (t f) -> p t f", t=DT)
        hmn = take(DT * HF).rearrange("p (t f) -> p t f", t=DT)
        pos[0] = 0
        ab2r = take(R * 2 * 512).rearrange("p (r c d) -> p r c d", r=R, c=2)
        g1 = [take(512) for _ in range(5)]
        g2 = [take(512) for _ in range(2)]
        x2ring = [take(XW + 1) for _ in range(NX)]
        GT = 4
        ost = take(GT * F).rearrange("p (t f) -> p t f", t=GT)
        xres = take(GT * F).rearrange("p (t f) -> p t f", t=GT)
        st6 = take(GT * 12).rearrange("p (t s) -> p t s", t=GT)
        mv = take(GT * 2).rearrange("p (t s) -> p t s", t=GT)

        names = """edges_in x_in qv_in bias_in consts x_zero code_ready pad_ready code_out runs_out ranks row_ready
        rows_in off_ready runs_in run_tr ed_ready flag_sum flag_tot flag_ready x_tr xt_ready wt_tr wt_ready wq_done
        wq_ready qk_done qk_ready oh c_done c_ready fb_built fb_used fb_done fb_free fb_c fb_evac
        t_done t_evac ones_in mk_step mk_cneg mk_ready mk_tr mk_red ab_ready ab_tr ab_rows ab_out
        e_ready e_max e2_free a_ready a_used g_done h_sum h_max o_sum h_lin h_exp h_ready h_tr ht_ready ht_free
        o_var o_std o_ready o_out chain pool_ready""".split()
        S = {n: sem(n) for n in names}
        w_in = [sem(f"w_in{i}") for i in range(2)]
        xr_out = [sem(f"xr_out{i}") for i in range(2)]
        xr_in = [sem(f"xr_in{i}") for i in range(NX)]
        ab_in = [sem(f"ab_in{i}") for i in range(R)]
        xres_in = sem("xres_in")

        class Layer:
            pass

        def layer(H, qv, wqk, qk, ks, mk, mx, ab, C, abd, n):
            v = Layer()
            v.H, v.qv, v.wqk, v.qk, v.ks, v.mk, v.mx, v.ab, v.C, v.abd, v.n = H, qv, wqk, qk, ks, mk, mx, ab, C, abd, n
            v.units = [[(r, h) for h in range(H)] for r in range(R)] if H > 1 else [[(r, 0) for r in range(R)]]
            return v

        L1 = layer(H, qv1, wqk1, qk1t, ks1, mk1, mx1, ab1, QC, ab_d, 0)
        L2 = layer(1, qv2, wqk2, qk2t, ks2, mk2, mx2, ab2, QC2, ab2_d, 1)
        WOFF = [0, 3, 6, 9]
        GROUPS = [(0, 4), (4, 7), (7, 10)]
        BASE = [0, 0, 6]
        NG1 = 4
        NST = NG1 * RS
        RING = NX
        PAIRS = NW // 2
        LOGITS_AT = R * KT + 2
        T_AT = LOGITS_AT + 1
        NB_X = 3 * KT

        def bank1(g, i):
            return ps[(DT * g + i) % 8]

        def ht_banks(g):
            return bank1(g + 1, DT), bank1(g + 1, DT + 1)

        def bank2(g, i, b):
            return ps[(BASE[g] + 2 * i + b) % 8]

        def group1(g):
            return g % 2, g // 2

        def store_out(sp, g):
            t0, t1 = GROUPS[g]
            for t in range(t0, t1):
                m = TAIL if t == NT - 1 else P
                sp.wait_ge(S["o_ready"], t + 1)
                sp.dma_start(out[t * P:t * P + m, :], ost[0:m, t - t0, :]).then_inc(S["o_out"], 16)

        def slot(n):
            return n % 2 if n < WOFF[3] else (n - WOFF[3]) % 2

        def landed(n):
            return w_in[slot(n)], 16 * sum(slot(m) == slot(n) for m in range(n + 1))

        def used(n):
            lay, r = n // 6, n % 3
            if n % 6 < 3:
                return S["wq_done"], (lay * R + r + 1) * KT
            return S["t_done"], (lay * R + r + 1) * NT

        block = ctx.enter_context(nc.Block())

        @block.sync
        def _(sp):
            for t, a in ((dsti, dst), (srci, src), (eti, etype)):
                sp.dma_start(t[0:EP, :], a.rearrange("(p c) -> p c", p=EP)).then_inc(S["edges_in"], 16)
            for q, k, t in ((q1, k1, qv1), (q2, k2, qv2)):
                h = t.shape[2] // 2
                sp.dma_start(t[:, :, 0:h], q.rearrange("(k p) h -> p k h", p=P), allow_slow_non_contiguous=True).then_inc(S["qv_in"], 16)
                sp.dma_start(t[:, :, h:2 * h], k.rearrange("(k p) h -> p k h", p=P), allow_slow_non_contiguous=True).then_inc(S["qv_in"], 16)
            sp.wait_ge(S["code_ready"], 1)
            sp.dma_start(code_d[0:E].rearrange("(p c) -> p c", p=EP), code[0:EP, :]).then_inc(S["code_out"], 16)
            sp.dma_start(code_d[E:E + PADL].rearrange("(a c) -> a c", a=1), f1[0:1, 0:PADL]).then_inc(S["code_out"], 16)
            sp.wait_ge(S["code_out"], 32)
            every = bass.AP(code_d.tensor, 0, [[GRAN, NROW], [1, RUNL]])
            sp.dma_start(runs_d[:, :], every).then_inc(S["runs_out"], 16)
            sp.wait_ge(S["x_zero"], 1)
            sp.dma_start(x_sb[:, 0:NT - 1, :], x[0:(NT - 1) * P, :].rearrange("(t p) f -> p t f", p=P)).then_inc(S["x_in"], 16)
            sp.dma_start(x_sb[0:TAIL, NT - 1, :], x[(NT - 1) * P:N, :]).then_inc(S["x_in"], 16)

            def load_w(n):
                if n >= 2 and n != 10:
                    sp.wait_ge(*used(min(n - 2, 8) if n < 11 else 9))
                w = (W1, W1, W2, W2)[n // 3][n % 3]
                sp.dma_start(wslot[slot(n)], w.rearrange("(k p) f -> p k f", p=P)).then_inc(w_in[slot(n)], 16)

            load_w(0)
            load_w(1)
            for t, a in ((b1b, b1), (b2b, b2)):
                sp.dma_start(t[:, :], a.rearrange("(a f) -> a f", a=1).broadcast_to([P, F])).then_inc(S["bias_in"], 16)
            for n in range(2, 5):
                load_w(n)

            def store_xr(lay):
                for n in range(RS):
                    sp.wait_ge(S["t_evac"], lay.n * RS + n + 1)
                    if lay is L1:
                        sp.dma_start(xr_d[n].rearrange("a p c -> p a c"), stg1[n % 2]).then_inc(xr_out[n % 2], 16)
                    else:
                        sp.dma_start(xr2_d[n], stg[n % 2][:, 0:XW]).then_inc(xr_out[n % 2], 16)
                    if n % NT == NT - 1:
                        if lay is L1:
                            load_w(5 + n // NT)
                        elif n == NT - 1:
                            load_w(11)

            def ab_store(lay):
                sp.wait_ge(S["ab_rows"], lay.n + 1)
                sp.dma_start(lay.abd[:, :], rows[0:lay.C, :]).then_inc(S["ab_out"], 16)
                sp.wait_ge(S["ab_out"], 16 * (lay.n + 1))
                for i in range(2):
                    sp.wait_ge(xr_out[i], 16 * (lay.n + 1) * RS // 2)

            store_xr(L1)
            load_w(8)
            ab_store(L1)
            sp.wait_ge(*used(8))

            def load_ab1(g, r):
                hp, dh = group1(g)
                c = r * 8 + hp * 4
                sp.dma_start(abr[:, r, :, :], ab_d[c:c + 4, dh * DH:(dh + 1) * DH].partition_broadcast(P)).then_inc(ab_in[r], 16)

            for r in range(R):
                load_ab1(0, r)
            for g in range(NG1):
                hp, dh = group1(g)
                for r in range(R):
                    with sp.Fori(0, NT // NX) as j:
                        for i in range(NX):
                            sp.wait_ge(S["a_used"], j * NX + ((g * R + r) * NT + i + 1))
                            sp.dma_start(xring[i], xr_d[bass.ds(j * NX + (r * NT + i), 1), hp].squeeze(0)).then_inc(xr_in[i], 16)
                    sp.wait_ge(S["e_ready"], (g * R + r + 1) * NT)
                    if g + 1 < NG1:
                        load_ab1(g + 1, r)
                    elif r == 1:
                        load_w(9)
            sp.wait_ge(S["a_used"], RING + NST)
            load_w(10)
            sp.wait_ge(S["h_tr"], 3 * NG1)
            store_xr(L2)
            ab_store(L2)
            sp.wait_ge(*used(11))

            def load_x(g):
                for t in range(*GROUPS[g]):
                    m = TAIL if t == NT - 1 else P
                    sp.dma_start(xres[0:m, t - GROUPS[g][0], :], x[t * P:t * P + m, :]).then_inc(xres_in, 16)

            def load_ab2(g, r):
                t0, t1 = GROUPS[g]
                w = (t1 - t0) * P
                sp.dma_start(ab2r[:, r, :, 0:w], ab2_d[r * 2:r * 2 + 2, t0 * P:t1 * P].partition_broadcast(P)).then_inc(ab_in[r], 16)

            for r in range(R):
                load_ab2(0, r)
            for g, (t0, t1) in enumerate(GROUPS):
                for r in range(R):
                    with sp.Fori(0, NT // NX) as j:
                        for i in range(NX):
                            sp.wait_ge(S["a_used"], j * NX + (NST + (g * R + r) * NT + i + 1))
                            sp.dma_start(x2ring[i][:, 0:XW], xr2_d[bass.ds(j * NX + (r * NT + i), 1)].squeeze(0)).then_inc(xr_in[i], 16)
                    if g + 1 < len(GROUPS):
                        sp.wait_ge(S["e_ready"], NST + (g * R + r + 1) * NT)
                        load_ab2(g + 1, r)
                    if (g, r) == (0, 0):
                        load_x(0)
                if g:
                    store_out(sp, g - 1)
                    sp.wait_ge(S["o_out"], 16 * t0)
                    load_x(g)
            store_out(sp, len(GROUPS) - 1)
            sp.wait_ge(S["o_out"], 16 * NT)

        @block.gpsimd
        def _(pool):
            nc.gpsimd.memset(ident[:, :], 0.0).then_inc(S["pool_ready"], 1)
            pool.wait_ge(S["pool_ready"], 1)
            io = dict(allow_small_or_imprecise_dtypes=True)
            nc.gpsimd.affine_select(out=ident[:, :], in_=ident[:, :], compare_op=ALU.not_equal, fill=1.0,
                                    base=0, pattern=[[-1, P]], channel_multiplier=1).then_inc(S["consts"], 1)
            nc.gpsimd.iota(wrow, [[1, NW]], base=0, channel_multiplier=0, **io).then_inc(S["consts"], 1)
            nc.gpsimd.iota(small[:, 0:2], [[SW, 2]], base=0, channel_multiplier=1, **io).then_inc(S["consts"], 1)
            nc.gpsimd.memset(onesf[:, :], 1.0).then_inc(S["consts"], 1)
            nc.gpsimd.iota(wid, [[SW, 2], [0, RUN], [1, SW]], base=0, channel_multiplier=0, **io).then_inc(S["consts"], 1)
            nc.gpsimd.iota(i_m[:, :], [[1, WM]], base=0, channel_multiplier=0, **io).then_inc(S["consts"], 1)
            nc.gpsimd.iota(i_s[:, :], [[1, P]], base=0, channel_multiplier=0, **io).then_inc(S["consts"], 1)
            nc.gpsimd.memset(zm[:, :], 0.0).then_inc(S["consts"], 1)
            pool.wait_ge(S["code_out"], 32)
            pool.wait_ge(S["row_ready"], 1)
            for s in range(2):
                nc.gpsimd.indirect_dma_start(rowb[0:SW, s, :], None, code_d[0:E].rearrange("(p c) -> p c", c=EC),
                                             bass.IndirectOffsetOnAxis(smalli[0:SW, s:s + 1], 0)).then_inc(S["rows_in"], 16)
            pool.wait_ge(S["off_ready"], 1)
            pool.wait_ge(S["runs_out"], 16)
            for s in range(2):
                nc.gpsimd.indirect_dma_start(runb[0:SW, s, :], None, runs_d[:, :],
                                             bass.IndirectOffsetOnAxis(smalli[0:SW, 2 + s:3 + s], 0)).then_inc(S["runs_in"], 16)
            def ones(lay):
                for s in range(2):
                    if lay is L1:
                        last = nc.gpsimd.memset(stg1[s].rearrange("p a (h c) -> p a h c", h=2)[:, :, :, HD], 1.0)
                    else:
                        last = nc.gpsimd.memset(stg[s][:, HF:HF + 1], 1.0)
                last.then_inc(S["ones_in"], 1)

            pool.wait_ge(S["wq_done"], R * KT)
            ones(L1)
            for g in range(NG1 - 1):
                pool.wait_ge(S["h_sum"], DT * (g + 1))
                nc.gpsimd.tensor_scalar(hmn, hst, 0.0, None, ALU.min).then_inc(S["h_lin"], 1)
                nc.gpsimd.tensor_scalar(hst, hst, 0.0, -1.0, ALU.max, ALU.add).then_inc(S["h_max"], 1)
                pool.wait_ge(S["h_max"], g + 1)
                pool.wait_ge(S["h_exp"], g + 1)
                nc.gpsimd.tensor_tensor(hst, hst, hmn, ALU.add).then_inc(S["h_ready"], 1)
            pool.wait_ge(S["h_tr"], 3 * NG1)
            ones(L2)

        @block.scalar
        def _(act):
            copy = ACT.Copy
            n = 0
            for kt in range(KT):
                for t0 in range(0, NT, 4):
                    w = min(4, NT - t0) * P
                    act.wait_ge(S["x_tr"], n + 1)
                    nc.scalar.activation(xT[:, kt, t0 * P:t0 * P + w], ps[n % 2][:, 0:w], copy).then_inc(S["xt_ready"], 1)
                    n += 1

            def wq_out(lay, i):
                act.wait_ge(S["wq_done"], lay.n * R * KT + i + 1)
                r, kt = i // KT, i % KT
                o = lay.wqk[:, kt, :].rearrange("p (a r h) -> p a r h", a=2, r=R)[:, :, r, :]
                nc.scalar.activation(o, ps[6 + i % 2][:, 0:2 * lay.H].rearrange("p (a h) -> p a h", a=2), copy).then_inc(S["wq_ready"], 1)

            def wt_out(lay, i):
                act.wait_ge(S["wt_tr"], lay.n * R * KT + i + 1)
                if i >= 2:
                    act.wait_ge(S["wq_done"], lay.n * R * KT + i - 1)
                for b in range(2):
                    last = nc.scalar.activation(WT[i % 2][:, b * HF:(b + 1) * HF], ps[2 + 2 * (i % 2) + b][:, 0:HF], copy)
                last.then_inc(S["wt_ready"], 1)

            def logits(lay):
                act.wait_ge(S["qk_done"], lay.n + 1)
                v = ps[6][:, 0:NT * lay.C].rearrange("p (t c) -> p t c", t=NT)
                nc.scalar.activation(lay.qk[:, :, :], v, copy)
                nc.scalar.activation(lay.ks[:, :, :], v[:, :, lay.C // 2:], copy, scale=SLOPE).then_inc(S["qk_ready"], 1)

            def transform_out(lay, n):
                if n == 0:
                    act.wait_ge(S["ones_in"], lay.n + 1)
                act.wait_ge(S["t_done"], lay.n * RS + n + 1)
                if n >= 2:
                    act.wait_ge(xr_out[n % 2], 16 * (lay.n * RS // 2 + n // 2))
                for b in range(2):
                    bank = ps[2 + 2 * (n % 2) + b][:, 0:HF]
                    if lay is L1:
                        o = stg1[n % 2][:, b, :].rearrange("p (h c) -> p h c", h=2)[:, :, 0:HD]
                        last = nc.scalar.activation(o, bank.rearrange("p (h c) -> p h c", h=2), copy)
                    else:
                        last = nc.scalar.activation(stg[n % 2][:, b * (HF + 1):b * (HF + 1) + HF], bank, copy)
                last.then_inc(S["t_evac"], 1)

            act.sem_inc(S["c_ready"], 2)
            for pair in range(PAIRS):
                act.wait_ge(S["c_done"], pair + 3)
                for c in range(2):
                    d = (2 * pair + c) * WIN
                    last = nc.scalar.activation(Ct[:, :, d:d + WIN], ps[pair % 2][:, c * WM:(c + 1) * WM].rearrange("p (a b) -> p a b", b=WIN), copy)
                last.then_inc(S["c_ready"], 1)
                k = pair - 1
                if 0 <= k < R * KT:
                    wt_out(L1, k)
                if 0 <= k - 2 < R * KT:
                    wq_out(L1, k - 2)
                if k == LOGITS_AT:
                    logits(L1)
                if k >= T_AT and (k - T_AT) % KT == KT - 1:
                    transform_out(L1, (k - T_AT) // KT)

            def transform(lay, n0):
                for n in range(n0, RS):
                    transform_out(lay, n)

            def ab_rows(lay):
                act.wait_ge(S["ab_tr"], lay.n + 1)
                for b in range(3):
                    w = min(512, NP - 512 * b)
                    last = nc.scalar.activation(rows[0:lay.C, b * 512:b * 512 + w], ps[(0, 1, 6)[b]][0:lay.C, 0:w], copy)
                last.then_inc(S["ab_rows"], 1)

            transform(L1, (PAIRS - 1 - T_AT) // KT)
            for i in range(2):
                act.wait_ge(xr_out[i], 16 * RS // 2)
            for i in range(R * KT + 1):
                if i < R * KT:
                    wt_out(L2, i)
                if i:
                    wq_out(L2, i - 1)
            ab_rows(L1)

            def ht_out(g, c):
                hp, dh = group1(g)
                a, b = ht_banks(g)
                act.wait_ge(S["h_tr"], 3 * g + c + 1)
                nc.scalar.activation(xT[:, hp * 3 + c, dh * DH:dh * DH + 512], a[:, :], copy)
                nc.scalar.activation(xT[:, hp * 3 + c, dh * DH + 512:(dh + 1) * DH], b[:, 0:DH - 512], copy).then_inc(S["ht_ready"], 1)

            def exp_min(g):
                act.wait_ge(S["h_lin"], g + 1)
                nc.scalar.activation(hmn, hmn, ACT.Exp).then_inc(S["h_exp"], 1)

            for g in range(NG1):
                hp, dh = group1(g)
                for r in range(R):
                    act.wait_ge(ab_in[r], 16 * (g + 1))
                    for t in range(NT):
                        step = g * RS + r * NT + t
                        act.wait_ge(S["a_used"], step + 1)
                        act.wait_ge(S["e2_free"], step + 1)
                        for h in range(2):
                            col = r * H + hp * 2 + h
                            nc.scalar.activation(e1[t % 5][:, h, :], abr[:, r, h, :], ACT.Exp, bias=qk1t[:, t, col + R * H:col + R * H + 1])
                            last = nc.scalar.activation(e2[t % 2][:, h, :], abr[:, r, 2 + h, :], ACT.Exp, bias=ks1[:, t, col:col + 1])
                        last.then_inc(S["e_ready"], 1)
                        if (r, t) == (0, 4) and g >= 2:
                            ht_out(g - 2, 2)
                        if (r, t) == (0, 7) and g:
                            exp_min(g - 1)
                        if (r, t) == (2, 4) and g:
                            ht_out(g - 1, 0)
                            ht_out(g - 1, 1)
            ht_out(NG1 - 2, 2)
            exp_min(NG1 - 1)
            for c in range(3):
                ht_out(NG1 - 1, c)
            logits(L2)
            transform(L2, 0)
            ab_rows(L2)
            def deviations(g):
                m = GROUPS[g][1] - GROUPS[g][0]
                act.wait_ge(S["o_var"], g + 1)
                nc.scalar.activation(mv[:, 0:m, 1], mv[:, 0:m, 1], ACT.Sqrt).then_inc(S["o_std"], 1)

            for g, (t0, t1) in enumerate(GROUPS):
                w = (t1 - t0) * P
                for r in range(R):
                    act.wait_ge(ab_in[r], 16 * (NG1 + g + 1))
                    for t in range(NT):
                        step = NST + g * RS + r * NT + t
                        act.wait_ge(S["a_used"], step + 1)
                        act.wait_ge(S["e2_free"], step + 1)
                        nc.scalar.activation(g1[t % 5][:, 0:w], ab2r[:, r, 0, 0:w], ACT.Exp, bias=qk2t[:, t, R + r:R + r + 1])
                        nc.scalar.activation(g2[t % 2][:, 0:w], ab2r[:, r, 1, 0:w], ACT.Exp, bias=ks2[:, t, r:r + 1]).then_inc(S["e_ready"], 1)
                        if (r, t) == (1, 9) and g:
                            deviations(g - 1)
            deviations(len(GROUPS) - 1)

        @block.tensor
        def _(pe):
            mm = nc.tensor.matmul
            pe.wait_ge(S["consts"], 8)
            pe.wait_ge(S["ranks"], 1)
            for s in range(2):
                last = mm(ps[7][0:SW, s:s + 1], G[0:EP, s * SW:(s + 1) * SW], onesf[0:EP, 0:1], start=True, stop=True)
            last.then_inc(S["ranks"], 1)
            pe.wait_ge(S["x_in"], 32)
            n = 0
            for kt in range(KT):
                for t0 in range(0, NT, 4):
                    if n >= 2:
                        pe.wait_ge(S["xt_ready"], n - 1)
                    for t in range(t0, min(t0 + 4, NT)):
                        last = nc.tensor.transpose(ps[n % 2][:, (t - t0) * P:(t - t0 + 1) * P], x_sb[:, t, kt * P:(kt + 1) * P], ident[:, :])
                    last.then_inc(S["x_tr"], 1)
                    n += 1

            def wt_transposes(lay, i):
                r, kt = i // KT, i % KT
                n = WOFF[2 * lay.n] + r
                if kt == 0:
                    pe.wait_ge(*landed(n))
                if i >= 2:
                    pe.wait_ge(S["wt_ready"], lay.n * R * KT + i - 1)
                elif lay is L2:
                    pe.wait_ge(S["t_evac"], RS)
                for ft in range(KT):
                    last = nc.tensor.transpose(ps[2 + 2 * (i % 2) + ft // 3][:, (ft % 3) * P:(ft % 3 + 1) * P],
                                               wslot[slot(n)][:, kt, ft * P:(ft + 1) * P], ident[:, :])
                last.then_inc(S["wt_tr"], 1)

            def wq_product(lay, i):
                pe.wait_ge(S["wt_ready"], lay.n * R * KT + i + 1)
                if i >= 2:
                    pe.wait_ge(S["wq_ready"], lay.n * R * KT + i - 1)
                elif lay is L1:
                    pe.wait_ge(S["flag_ready"], 1)
                    pe.wait_ge(S["qv_in"], 64)
                else:
                    pe.wait_ge(S["mk_red"], NT)
                for ft in range(KT):
                    last = mm(ps[6 + i % 2][:, 0:2 * lay.H], WT[i % 2][:, ft * P:(ft + 1) * P], lay.qv[:, ft, :],
                              start=ft == 0, stop=ft == KT - 1)
                last.then_inc(S["wq_done"], 1)

            def logits(lay):
                pe.wait_ge(S["wq_ready"], (lay.n + 1) * R * KT)
                for t in range(NT):
                    for kt in range(KT):
                        last = mm(ps[6][:, t * lay.C:(t + 1) * lay.C], xT[:, kt, t * P:(t + 1) * P], lay.wqk[:, kt, :],
                                  start=kt == 0, stop=kt == KT - 1)
                last.then_inc(S["qk_done"], 1)

            def transform_tile(lay, r, t, kt):
                n = WOFF[2 * lay.n + 1] + r
                i = lay.n * RS + r * NT + t
                if kt == 0:
                    if t == 0:
                        pe.wait_ge(*landed(n))
                    if r * NT + t >= 2:
                        pe.wait_ge(S["t_evac"], i - 1)
                    elif lay is L1:
                        pe.wait_ge(S["wt_ready"], R * KT)
                for b in range(2):
                    last = mm(ps[2 + 2 * (t % 2) + b][:, 0:HF], xT[:, kt, t * P:(t + 1) * P],
                              wslot[slot(n)][:, kt, b * HF:(b + 1) * HF], start=kt == 0, stop=kt == KT - 1)
                if kt == KT - 1:
                    last.then_inc(S["t_done"], 1)

            def transform(lay, r, t0=0):
                for t in range(t0, NT):
                    for kt in range(KT):
                        transform_tile(lay, r, t, kt)

            pe.wait_ge(S["runs_in"], 32)
            for s in range(2):
                for t in range(RUN):
                    c = (s * RUN + t) * SW
                    last = nc.tensor.transpose(ps[7][:, c:c + SW], runb[0:SW, s, t * P:(t + 1) * P], ident[0:SW, 0:SW])
            last.then_inc(S["run_tr"], 1)
            pe.wait_ge(S["flag_sum"], 1)
            mm(ps[7][0:1, 0:1], small[:, 8:9], onesf[:, 0:1], start=True, stop=True).then_inc(S["flag_tot"], 1)
            pe.sem_inc(S["c_done"], 2)
            pe.wait_ge(S["xt_ready"], NB_X)
            for pair in range(PAIRS):
                h = pair % 2
                pe.wait_ge(S["oh"], pair + 1)
                pe.wait_ge(S["c_ready"], pair + 1)
                for c in range(2):
                    for t in range(RUN):
                        n = (h * 2 + c) * RUN + t
                        last = mm(ps[h][:, c * WM:(c + 1) * WM], ohs[n], ohm[n], start=t == 0, stop=t == RUN - 1)
                last.then_inc(S["c_done"], 1)
                if pair < R * KT:
                    wt_transposes(L1, pair)
                if 0 <= pair - 2 < R * KT:
                    wq_product(L1, pair - 2)
                if pair == LOGITS_AT:
                    logits(L1)
                if pair >= T_AT:
                    transform_tile(L1, 0, (pair - T_AT) // KT, (pair - T_AT) % KT)
            pe.wait_ge(S["flag_ready"], 1)
            held = pe.value_load(smalli[0:1, 4:5], min_val=0, max_val=E)
            with pe.If(held < E):
                pe.wait_ge(S["c_ready"], NW // 2 + 2)
                with pe.Fori(0, NW) as w:
                    pe.wait_ge(S["fb_free"], w + 1)
                    mm(ps[0][:, 0:WM], zm[:, 0:P], zm[:, 0:WM], start=True, stop=False, skip_group_check=True)
                    with pe.Fori(0, EC // 4) as j:
                        pe.wait_ge(S["fb_built"], w * (EC // 4) + j + 1)
                        for t in range(4):
                            last = mm(ps[0][:, 0:WM], ohs[t][0:EP, :], ohm[t][0:EP, :], start=False, stop=True, skip_group_check=True)
                        last.then_inc(S["fb_used"], 1)
                    last = mm(ps[0][:, 0:WM], zm[:, 0:P], zm[:, 0:WM], start=False, stop=True, skip_group_check=True)
                    last.then_inc(S["fb_done"], 1)
                pe.wait_ge(S["fb_evac"], NW)

            def mk_transposes(lay, u):
                u0 = u if lay is L1 else R
                pe.wait_ge(S["mk_step"], (u + 1) * NT * H if lay is L1 else RS * (H + 1))
                for t in range(NT):
                    i = u0 * NT + t
                    if i >= 2:
                        pe.wait_ge(S["mk_red"], i - 1)
                    for c in range(len(lay.units[u])):
                        last = nc.tensor.transpose(ps[6 + i % 2][:, c * P:(c + 1) * P], Mk[u0 % 2][:, c, t * P:(t + 1) * P], ident[:, :])
                    last.then_inc(S["mk_tr"], 1)

            def ab_transposes(lay):
                pe.wait_ge(S["ab_ready"], lay.n + 1)
                pe.wait_ge(S["wq_ready"], 2 * R * KT)
                for t in range(NT):
                    last = nc.tensor.transpose(ps[(0, 1, 6)[t // 4]][0:lay.C, (t % 4) * P:(t % 4 + 1) * P], lay.ab[:, t, :], ident[:, :])
                last.then_inc(S["ab_tr"], 1)

            for kt in range((PAIRS - T_AT) % KT, KT) if (PAIRS - T_AT) % KT else ():
                transform_tile(L1, 0, (PAIRS - T_AT) // KT, kt)
            transform(L1, 0, -(-(PAIRS - T_AT) // KT))
            transform(L1, 1)
            transform(L1, 2)
            mk_transposes(L1, 0)
            wt_transposes(L2, 0)
            for i in range(R * KT):
                if i + 1 < R * KT:
                    wt_transposes(L2, i + 1)
                wq_product(L2, i)
            pe.wait_ge(S["wq_ready"], 2 * R * KT)
            mk_transposes(L1, 1)
            mk_transposes(L1, 2)
            ab_transposes(L1)

            def h_transposes(g, c):
                a, b = ht_banks(g)
                pe.wait_ge(S["h_ready"], g + 1)
                if 3 * g + c:
                    pe.wait_ge(S["ht_ready"], 3 * g + c)
                for t in range(DT):
                    last = nc.tensor.transpose((a, b)[t // 4][:, (t % 4) * P:(t % 4 + 1) * P], hst[:, t, c * P:(c + 1) * P], ident[:, :])
                last.then_inc(S["h_tr"], 1)

            pe.sem_inc(S["a_used"], RING)
            pe.wait_ge(S["ab_rows"], 1)
            pe.wait_ge(S["wt_ready"], 2 * R * KT)
            for g in range(NG1):
                if g >= 2:
                    h_transposes(g - 2, 2)
                    pe.wait_ge(S["ht_ready"], 3 * (g - 1))
                for i in range(DT):
                    if g and i >= 3:
                        pe.wait_ge(S["h_sum"], DT * (g - 1) + i - 2)
                    mm(bank1(g, i)[:, 0:XB], zm[:, 0:P], zm[:, 0:XB], start=True, stop=False, skip_group_check=True)

                def step(r, t):
                    pe.wait_ge(S["a_ready"], r * NT + (g * RS + t + 1))
                    pe.wait_ge(xr_in[t % NX], r * (16 * NT // NX) + 16 * (g * RS // NX + t // NX + 1))
                    for h in range(2):
                        for i in range(DT):
                            o = h * (HD + 1)
                            last = mm(bank1(g, i)[:, o:o + HD + 1], e1[t % 5][:, h, i * P:(i + 1) * P], xring[t % NX][:, o:o + HD + 1],
                                      start=False, stop=True, skip_group_check=True)
                    last.then_inc(S["a_used"], 1)

                with pe.Fori(0, R - 1) as r:
                    for t in range(NT):
                        step(r, t)
                if g:
                    h_transposes(g - 1, 0)
                    h_transposes(g - 1, 1)
                for t in range(NT):
                    step(R - 1, t)
            h_transposes(NG1 - 2, 2)
            for c in range(3):
                h_transposes(NG1 - 1, c)

            pe.wait_ge(S["ht_ready"], 3 * NG1)
            logits(L2)
            transform(L2, 0)
            transform(L2, 1)
            mk_transposes(L2, 0)
            for t in range(NT):
                if t == NT // 2:
                    ab_transposes(L2)
                for kt in range(KT):
                    transform_tile(L2, 2, t, kt)
            pe.wait_ge(S["ab_rows"], 2)
            pe.wait_ge(S["t_evac"], 2 * RS)
            for g, (t0, t1) in enumerate(GROUPS):
                for i in range(t1 - t0):
                    if g:
                        pe.wait_ge(S["o_sum"], GROUPS[g - 1][0] + (i + 1 if g == 1 else max(i, 1)))
                    for b in range(2):
                        mm(bank2(g, i, b)[:, 0:HF + 1], zm[:, 0:P], zm[:, 0:HF + 1], start=True, stop=False, skip_group_check=True)
                with pe.Fori(0, R) as r:
                    for t in range(NT):
                        pe.wait_ge(S["a_ready"], r * NT + (NST + g * RS + t + 1))
                        pe.wait_ge(xr_in[t % NX], r * (16 * NT // NX) + 16 * ((NST + g * RS) // NX + t // NX + 1))
                        for i in range(t1 - t0):
                            a = g1[t % 5][:, i * P:(i + 1) * P]
                            mm(bank2(g, i, 0)[:, 0:HF + 1], a, x2ring[t % NX][:, 0:HF + 1], start=False, stop=True, skip_group_check=True)
                            last = mm(bank2(g, i, 1)[:, 0:HF], a, x2ring[t % NX][:, HF + 1:XW], start=False, stop=True, skip_group_check=True)
                        last.then_inc(S["a_used"], 1)

        @block.vector
        def _(dve):
            V = nc.vector
            links = [0]

            def link(ins):
                links[0] += 1
                ins.then_inc(S["chain"], 1)
                dve.wait_ge(S["chain"], links[0])

            V.memset(x_sb[:, NT - 1, :], 0.0).then_inc(S["x_zero"], 1)
            V.memset(f1[0:1, 0:PADL], float(2047 * CODE_DST)).then_inc(S["chain"], 1)
            links[0] += 1
            dve.wait_ge(S["edges_in"], 48)
            link(V.scalar_tensor_tensor(tmpf[0:EP, :], eti[0:EP, :], float(CODE_TYPE), srci[0:EP, :], ALU.mult, ALU.add))
            link(V.scalar_tensor_tensor(code[0:EP, :], dsti[0:EP, :], float(CODE_DST), tmpf[0:EP, :], ALU.mult, ALU.add))
            dve.sem_inc(S["code_ready"], 1)
            dve.wait_ge(S["consts"], 8)
            link(V.tensor_scalar(wrow, wrow, float(WIN * CODE_DST), None, ALU.mult))
            link(V.tensor_scalar(small[:, 2:4], small[:, 0:2], float(WIN * CODE_DST), None, ALU.mult))
            V.tensor_scalar(G[0:EP, :], wrow[0:EP, :], code[0:EP, 0:1], None, ALU.is_gt).then_inc(S["ranks"], 1)
            dve.wait_ge(S["ranks"], 2)
            link(V.tensor_scalar(small[0:SW, 4:6], ps[7][0:SW, 0:2], -1.0, 0.0, ALU.add, ALU.max))
            V.tensor_copy(smalli[0:SW, 0:2], small[0:SW, 4:6]).then_inc(S["row_ready"], 1)
            dve.wait_ge(S["rows_in"], 32)
            for s in range(2):
                link(V.tensor_scalar(tmpf[0:SW, :], rowb[0:SW, s, :], small[0:SW, 2 + s:3 + s], 0.0, ALU.is_lt, ALU.add,
                                     accum_out=small[0:SW, 6 + s:7 + s]))
            link(V.scalar_tensor_tensor(small[0:SW, 10:12], small[0:SW, 4:6], float(EC), small[0:SW, 6:8], ALU.mult, ALU.add))
            link(V.tensor_scalar(small[0:SW, 10:12], small[0:SW, 10:12], float(E - 1), None, ALU.min))
            link(V.tensor_copy(smalli[0:SW, 2:4], small[0:SW, 10:12]))
            V.tensor_scalar(smalli[0:SW, 2:4], smalli[0:SW, 2:4], GRAN.bit_length() - 1, None, ALU.logical_shift_right).then_inc(S["off_ready"], 1)

            def unpack(codes, p, n, dsth, dstl, rs, t0, t1, slo_o):
                link(V.tensor_scalar(t0, codes, P - 1, None, ALU.bitwise_and))
                link(V.tensor_copy(slo_o, t0))
                link(V.tensor_scalar(t0, codes, 7, 63, ALU.logical_shift_right, ALU.bitwise_and))
                link(V.tensor_scalar(t1, codes, 11, 3, ALU.logical_shift_right, ALU.bitwise_and))
                link(V.scalar_tensor_tensor(rs, t1, float(NT - 16), t0, ALU.mult, ALU.add))
                link(V.tensor_scalar(t0, codes, 13, WIN - 1, ALU.logical_shift_right, ALU.bitwise_and))
                link(V.scalar_tensor_tensor(rs, rs, float(WIN), t0, ALU.mult, ALU.add))
                link(V.tensor_scalar(t0, codes, 16, None, ALU.logical_shift_right))
                link(V.tensor_copy(dsth, t0))

            dve.wait_ge(S["run_tr"], 1)
            link(V.tensor_copy(edi, ps[7][:, 0:NE]))
            unpack(edi, P, NE, f0, None, f1, u0, u1, slo)
            link(V.tensor_tensor(f0, f0, wid, ALU.is_equal))
            link(V.scalar_tensor_tensor(mcode, f1, 1.0, f0, ALU.add, ALU.mult))
            link(V.tensor_scalar(mcode, mcode, -1.0, None, ALU.add))
            dve.sem_inc(S["ed_ready"], 1)
            V.reduce_sum(small[:, 8:9], f0, AX).then_inc(S["flag_sum"], 1)
            dve.wait_ge(S["flag_tot"], 1)
            V.tensor_copy(smalli[0:1, 4:5], ps[7][0:1, 0:1]).then_inc(S["flag_ready"], 1)
            with dve.Fori(0, 2) as s:
                with dve.Fori(0, SW // 4) as j:
                    for h in range(2):
                        dve.wait_ge(S["c_done"], s * (SW // 2) + j * 2 + (h + 1))
                        for c in range(2):
                            for t in range(RUN):
                                col = s * (RUN * SW) + j * 4 + (t * SW + h * 2 + c)
                                V.tensor_scalar(ohs[(h * 2 + c) * RUN + t], i_s[:, :], slo[:, bass.ds(col, 1)], None, ALU.is_equal)
                                last = V.tensor_scalar(ohm[(h * 2 + c) * RUN + t], i_m[:, :], mcode[:, bass.ds(col, 1)], None, ALU.is_equal)
                        last.then_inc(S["oh"], 1)
            dve.wait_ge(S["c_ready"], NW // 2 + 2)
            dve.wait_ge(S["flag_ready"], 1)
            held = dve.value_load(smalli[0:1, 4:5], min_val=0, max_val=E)
            with dve.If(held < E):
                before = links[0]
                nat = edi[0:EP, 0:EC]
                link(V.tensor_copy(nat, code[0:EP, :]))
                unpack(nat, EP, EC, f0[0:EP, 0:EC], None, f1[0:EP, 0:EC], u0[0:EP, 0:EC], u1[0:EP, 0:EC], slo[0:EP, 0:EC])
                dve.sem_inc(S["fb_used"], 1)
                with dve.Fori(0, NW) as w:
                    dve.sem_inc(S["fb_free"], 1)
                    V.tensor_scalar(wid[0:EP, 0:EC], f0[0:EP, 0:EC], float(WIN * CODE_DST), wrow[0:EP, bass.ds(w, 1)], ALU.mult, ALU.is_equal).then_inc(S["fb_c"], 1)
                    dve.wait_ge(S["fb_c"], w * 2 + 1)
                    V.scalar_tensor_tensor(mcode[0:EP, 0:EC], f1[0:EP, 0:EC], 1.0, wid[0:EP, 0:EC], ALU.add, ALU.mult).then_inc(S["fb_c"], 1)
                    with dve.Fori(0, EC // 4) as j:
                        dve.wait_ge(S["fb_c"], w * 2 + 2)
                        dve.wait_ge(S["fb_used"], w * (EC // 4) + j + 1)
                        for t in range(4):
                            V.tensor_scalar(ohs[t][0:EP, :], i_s[0:EP, :], slo[0:EP, bass.ds(j * 4 + t, 1)], None, ALU.is_equal)
                            last = V.tensor_scalar(ohm[t][0:EP, :], i_m[0:EP, :], 1.0, mcode[0:EP, bass.ds(j * 4 + t, 1)], ALU.add, ALU.is_equal)
                        last.then_inc(S["fb_built"], 1)
                    dve.wait_ge(S["fb_done"], w + 1)
                    V.tensor_copy(Ct[:, :, bass.ds(w * WIN, WIN)], ps[0][:, 0:WM].rearrange("p (a b) -> p a b", b=WIN)).then_inc(S["fb_evac"], 1)
                    dve.wait_ge(S["fb_evac"], w + 1)
                fb_links = links[0] - before
            with dve.Else():
                dve.sem_inc(S["chain"], fb_links)

            steps = [0]
            ends = []

            def maxima(lay, u):
                u0 = u if lay is L1 else R
                cols = lay.units[u]
                m = Mk[u0 % 2]
                started = {}

                def mask(i):
                    if i >= 2:
                        dve.wait_ge(S["mk_step"], ends[i - 2])
                    V.tensor_scalar(cneg[i % 2], Ct[:, i % RS, :], 0.0, -BIG, ALU.is_equal, ALU.mult).then_inc(S["mk_cneg"], 1)

                for r in sorted({r for r, _ in cols}):
                    for t in range(NT):
                        i = lay.n * RS + r * NT + t
                        if t == 0 and r == cols[0][0]:
                            mask(i)
                        if i + 1 < (2 if lay is L2 else 1) * RS and (t < NT - 1 or r < cols[-1][0]):
                            mask(i + 1)
                        dve.wait_ge(S["mk_cneg"], i + 1)
                        for c, (rr, h) in enumerate(cols):
                            if rr != r:
                                continue
                            k = lay.qk[:, t, R * lay.H + r * lay.H + h:R * lay.H + r * lay.H + h + 1]
                            if t == 0:
                                last = V.tensor_scalar(m[:, c, :], cneg[i % 2], k, None, ALU.add)
                            else:
                                dve.wait_ge(S["mk_step"], started[c])
                                last = V.scalar_tensor_tensor(m[:, c, 0:N], cneg[i % 2][:, 0:N], k, m[:, c, 0:N], ALU.add, ALU.max)
                            steps[0] += 1
                            started[c] = steps[0]
                            last.then_inc(S["mk_step"], 1)
                        ends.append(steps[0])

            def reduce(lay, u):
                u0 = u if lay is L1 else R
                n = len(lay.units[u])
                for t in range(NT):
                    i = u0 * NT + t
                    dve.wait_ge(S["mk_tr"], i + 1)
                    o = lay.mk[:, t, u, :] if lay is L1 else lay.mk[:, t, :, 0]
                    V.reduce_max(o, ps[6 + i % 2][:, 0:n * P].rearrange("p (c s) -> p c s", c=n), AX).then_inc(S["mk_red"], 1)

            def shifts(lay):
                dve.wait_ge(S["mk_red"], (R if lay is L1 else R + 1) * NT)
                H_ = lay.H
                q = lay.qk[:, :, 0:R * H_].rearrange("p t (r h) -> p t r h", r=R)
                k = lay.mk
                m, n, o = lay.mx[:, 0], lay.mx[:, 1], lay.mx[:, 2]
                link(V.tensor_tensor(m, q[:, :, 0, :], k[:, :, 0, :], ALU.add))
                for r in range(1, R):
                    link(V.tensor_tensor(n, q[:, :, r, :], k[:, :, r, :], ALU.add))
                    link(V.tensor_tensor(m, m, n, ALU.max))
                link(V.tensor_scalar(n, m, -BIG / 2, None, ALU.is_gt))
                link(V.scalar_tensor_tensor(o, m, SLOPE, m, ALU.mult, ALU.max))
                link(V.tensor_tensor(m, o, n, ALU.mult))
                w = min(2, H_)
                for r in range(R):
                    for hp in range(H_ // w):
                        c = (r * (H_ // w) + hp) * 2 * w
                        qq, mm_ = q[:, :, r, hp * w:(hp + 1) * w], m[:, :, hp * w:(hp + 1) * w]
                        V.tensor_tensor(lay.ab[:, :, c:c + w], qq, mm_, ALU.subtract)
                        last = V.scalar_tensor_tensor(lay.ab[:, :, c + w:c + 2 * w], qq, SLOPE, mm_, ALU.mult, ALU.subtract)
                last.then_inc(S["ab_ready"], 1)

            dve.wait_ge(S["c_ready"], NW // 2 + 2)
            dve.wait_ge(S["qk_ready"], 1)
            maxima(L1, 0)
            maxima(L1, 1)
            reduce(L1, 0)
            maxima(L1, 2)
            reduce(L1, 1)
            reduce(L1, 2)
            shifts(L1)

            dve.sem_inc(S["e2_free"], 2)
            dve.wait_ge(S["bias_in"], 32)

            def attention1(g, r, t):
                hp, dh = group1(g)
                step = r * NT + (g * RS + t)
                dve.wait_ge(S["e_ready"], step + 1)
                V.tensor_tensor(e1[t % 5], e1[t % 5], e2[t % 2], ALU.max).then_inc(S["e2_free"], 1)
                dve.wait_ge(S["e2_free"], step + 3)
                cc = Ct[:, r * NT + t, dh * DH:(dh + 1) * DH].unsqueeze(1) if isinstance(r, int) else \
                    Ct[:, bass.ds(r * NT + t, 1), dh * DH:(dh + 1) * DH]
                V.scalar_tensor_tensor(e1[t % 5], e1[t % 5], 1.0, cc.broadcast_to([P, 2, DH]), ALU.min, ALU.mult).then_inc(S["a_ready"], 1)

            def rows1(g):
                hp, dh = group1(g)
                dve.wait_ge(S["a_used"], RING + (g + 1) * RS)
                if g:
                    dve.wait_ge(S["h_tr"], 3 * g)
                z = small[:, 16:16 + 2 * DT].rearrange("p (t h) -> p t h", h=2)
                for i in range(DT):
                    link(V.tensor_scalar(z[:, i, :], bank1(g, i)[:, 0:XB].rearrange("p (h c) -> p h c", h=2)[:, :, HD], Z_EPS, None, ALU.add))
                    link(V.reciprocal(z[:, i, :], z[:, i, :]))
                    for h in range(2):
                        o = h * (HD + 1)
                        last = V.scalar_tensor_tensor(hst[:, i, h * HD:(h + 1) * HD], bank1(g, i)[:, o:o + HD], z[:, i, h:h + 1],
                                                      b1b[:, hp * HF + h * HD:hp * HF + (h + 1) * HD], ALU.mult, ALU.add)
                    last.then_inc(S["h_sum"], 1)

            for g in range(NG1):
                for t in range(NT):
                    if t == 2 and g:
                        rows1(g - 1)
                    attention1(g, 0, t)
                with dve.Fori(1, R) as r:
                    for t in range(NT):
                        attention1(g, r, t)
            rows1(NG1 - 1)
            dve.wait_ge(S["h_sum"], DT * NG1)
            V.tensor_scalar(hmn, hst, 0.0, None, ALU.min).then_inc(S["h_lin"], 1)
            link(V.tensor_scalar(hst, hst, 0.0, -1.0, ALU.max, ALU.add))
            dve.wait_ge(S["h_exp"], NG1)
            V.tensor_tensor(hst, hst, hmn, ALU.add).then_inc(S["h_ready"], 1)

            dve.wait_ge(S["h_tr"], 3 * NG1)
            dve.wait_ge(S["qk_ready"], 2)
            maxima(L2, 0)
            reduce(L2, 0)
            shifts(L2)

            def attention2(g, r, t):
                t0, t1 = GROUPS[g]
                w = (t1 - t0) * P
                step = r * NT + (NST + g * RS + t)
                dve.wait_ge(S["e_ready"], step + 1)
                V.tensor_tensor(g1[t % 5][:, 0:w], g1[t % 5][:, 0:w], g2[t % 2][:, 0:w], ALU.max).then_inc(S["e2_free"], 1)
                dve.wait_ge(S["e2_free"], step + 3)
                cc = Ct[:, r * NT + t, t0 * P:t1 * P] if isinstance(r, int) else \
                    Ct[:, bass.ds(r * NT + t, 1), t0 * P:t1 * P].rearrange("p a d -> p (a d)")
                V.scalar_tensor_tensor(g1[t % 5][:, 0:w], g1[t % 5][:, 0:w], 1.0, cc, ALU.min, ALU.mult).then_inc(S["a_ready"], 1)

            def rows2(g):
                t0, t1 = GROUPS[g]
                dve.wait_ge(S["a_used"], RING + NST + (g + 1) * RS)
                if g:
                    dve.wait_ge(S["o_out"], 16 * t0)
                z = small[:, 16:16 + GT]
                for i in range(t1 - t0):
                    link(V.tensor_scalar(z[:, i:i + 1], bank2(g, i, 0)[:, HF:HF + 1], Z_EPS, None, ALU.add))
                    link(V.reciprocal(z[:, i:i + 1], z[:, i:i + 1]))
                    for b in range(2):
                        last = V.scalar_tensor_tensor(ost[:, i, b * HF:(b + 1) * HF], bank2(g, i, b)[:, 0:HF], z[:, i:i + 1],
                                                      b2b[:, b * HF:(b + 1) * HF], ALU.mult, ALU.add)
                    last.then_inc(S["o_sum"], 1)
                dve.wait_ge(S["o_sum"], t1)

            def residual(g):
                t0, t1 = GROUPS[g]
                dve.wait_ge(xres_in, 16 * t1)
                for i in range(t1 - t0):
                    k = TAIL if t0 + i == NT - 1 else P
                    link(V.tensor_tensor(ost[0:k, i, :], ost[0:k, i, :], xres[0:k, i, :], ALU.add))
                    for b in range(2):
                        last = V.bn_stats(st6[:, i, b * 6:(b + 1) * 6], ost[:, i, b * HF:(b + 1) * HF])
                    link(last)
                    last = V.bn_aggr(mv[:, i, :], st6[:, i, :])
                link(last)
                V.tensor_scalar(mv[:, 0:t1 - t0, 1], mv[:, 0:t1 - t0, 1], LN_EPS, None, ALU.add).then_inc(S["o_var"], 1)

            def normalise(g):
                t0, t1 = GROUPS[g]
                dve.wait_ge(S["o_std"], g + 1)
                link(V.reciprocal(mv[:, 0:t1 - t0, 1], mv[:, 0:t1 - t0, 1]))
                for i in range(t1 - t0):
                    V.tensor_scalar(ost[:, i, :], ost[:, i, :], mv[:, i, 0:1], mv[:, i, 1:2], ALU.subtract, ALU.mult).then_inc(S["o_ready"], 1)

            for g in range(len(GROUPS)):
                for t in range(NT):
                    if t == 2 and g:
                        rows2(g - 1)
                    attention2(g, 0, t)
                for t in range(NT):
                    attention2(g, 1, t)
                if g:
                    residual(g - 1)
                for t in range(NT):
                    if t == 5 and g:
                        normalise(g - 1)
                    attention2(g, 2, t)
            rows2(len(GROUPS) - 1)
            residual(len(GROUPS) - 1)
            normalise(len(GROUPS) - 1)


_INS = ["x", "src", "dst", "edge_type_3", "L0_gnn_W1", "L0_gnn_q1", "L0_gnn_k1", "L0_gnn_b1",
        "L0_gnn_W2", "L0_gnn_q2", "L0_gnn_k2", "L0_gnn_b2"]


def kernel(**inputs):
    import numpy as _np
    import concourse.bacc as _bacc
    from concourse import mybir as _mybir
    from concourse.bass_utils import run_bass_kernel_spmd as _run

    nc = _bacc.Bacc("TRN2", target_bir_lowering=False, num_devices=1)
    arrays, args = {}, []
    for name in _INS:
        a = _np.ascontiguousarray(inputs[name])
        arrays[f"in_{name}"] = a
        args.append(nc.dram_tensor(f"in_{name}", a.shape, _mybir.dt.from_np(a.dtype), kind="ExternalInput").ap())
    out = nc.dram_tensor("out", inputs["x"].shape, _mybir.dt.float32, kind="ExternalOutput").ap()
    rgat(nc, *args, out)
    r = _run(nc, [arrays], core_ids=[0])
    return r.results[0]["out"]
```

```python
from contextlib import ExitStack

import concourse.bass as bass
from concourse import mybir

P = 128
F32 = mybir.dt.float32
F32R = mybir.dt.float32r
BF16 = mybir.dt.bfloat16
I32 = mybir.dt.int32
U32 = mybir.dt.uint32
U16 = mybir.dt.uint16
ALU = mybir.AluOpType
ACT = mybir.ActivationFunctionType
AX = mybir.AxisListType.X

SLOPE = 0.2
Z_EPS = 1e-16
LN_EPS = 1e-5
BIG = 1e30
CODE_DST = 8192
CODE_TYPE = 2048
WIN = 8
RUN = 3
GRAN = 32


def rgat(nc, x, src, dst, etype, W1, q1, k1, b1, W2, q2, k2, b2, out):
    N, F = x.shape
    E = src.shape[0]
    R = W1.shape[0]
    H = q1.shape[1]
    HD = F // H
    KT = F // P
    NT = (N + P - 1) // P
    NP = NT * P
    TAIL = N - (NT - 1) * P
    RS = R * NT
    HP = H // 2
    QC = 2 * R * H
    QC2 = 2 * R
    HF = F // 2
    EP = 125
    EC = E // EP
    NW = NP // WIN
    SW = NW // 2
    WM = RS * WIN
    RUNL = RUN * P
    NROW = E // GRAN
    PADL = RUNL
    XB = 2 * (HD + 1)
    DH = NP // 2
    DT = NT // 2
    XW = F + 2
    assert EP * EC == E and R == 3 and H == 4 and WM * 2 <= 512 and NW <= 2 * P and HD * 2 == HF

    code_d = nc.dram_tensor("code_d", [E + PADL], F32).ap()
    runs_d = nc.dram_tensor("runs_d", [NROW, RUNL], F32).ap()
    xr_d = nc.dram_tensor("xr_d", [RS, 2, P, XB], F32).ap()
    xr2_d = nc.dram_tensor("xr2_d", [RS, P, XW], F32).ap()
    ab_d = nc.dram_tensor("ab_d", [QC, NP], F32).ap()
    ab2_d = nc.dram_tensor("ab2_d", [QC2, NP], F32).ap()

    with ExitStack() as ctx:
        def sb(name, shape, dt=F32):
            return ctx.enter_context(nc.sbuf_tensor(name, shape, dt))

        def sem(name):
            return ctx.enter_context(nc.semaphore(name))

        Ct = sb("Ct", [P, RS, NP], U16)
        xT = sb("xT", [P, KT, NP])
        ident = sb("ident", [P, P])
        onesf = sb("onesf", [P, 2])
        zm = sb("zm", [P, 512], BF16)
        i_m = sb("i_m", [P, WM], BF16)
        i_s = sb("i_s", [P, P], BF16)
        qv1 = sb("qv1", [P, KT, 2 * H])
        qv2 = sb("qv2", [P, KT, 2])
        wqk1 = sb("wqk1", [P, KT, QC])
        wqk2 = sb("wqk2", [P, KT, QC2])
        qk1t = sb("qk1t", [P, NT, QC])
        ks1 = sb("ks1", [P, NT, R * H])
        qk2t = sb("qk2t", [P, NT, QC2])
        ks2 = sb("ks2", [P, NT, R])
        mk1 = sb("mk1", [P, NT, R, H])
        mk2 = sb("mk2", [P, NT, R, 1])
        mx1 = sb("mx1", [P, 4, NT, H])
        mx2 = sb("mx2", [P, 4, NT, 1])
        ab1 = sb("ab1", [P, NT, QC])
        ab2 = sb("ab2", [P, NT, QC2])
        b1b = sb("b1b", [P, F])
        b2b = sb("b2b", [P, F])
        code = sb("code", [P, EC])
        small = sb("small", [P, 64])
        smalli = sb("smalli", [P, 8], U32)
        ARENA = 22432
        ar = sb("arena", [P, ARENA])
        arena_at = nc.sbuf_base - ARENA * 4
        ps = [ctx.enter_context(nc.psum_tensor(f"ps{i}", [P, 512], F32)) for i in range(8)]

        def cut(at, n):
            assert at + n <= ARENA, (at, n)
            return ar[:, at:at + n]

        WS = KT * F
        wslot = [cut(i * WS, WS).rearrange("p (k f) -> p k f", k=KT) for i in range(2)]
        pos = [2 * WS]

        def take(n):
            pos[0] += n
            return cut(pos[0] - n, n)

        dsti, srci, eti = (take(EC).bitcast(I32) for _ in range(3))
        tmpf = take(EC)
        rowb = take(2 * EC).rearrange("p (s c) -> p s c", s=2)
        runb = take(2 * RUNL).rearrange("p (s c) -> p s c", s=2)
        NE = 2 * RUN * SW
        edi = take(NE).bitcast(I32)
        u0, u1 = take(NE).bitcast(I32), take(NE).bitcast(I32)
        f0, f1 = take(NE), take(NE)
        wid = take(NE)
        wrow = take(NW)
        G = take(NW)
        slo = take(NE)
        mcode = take(NE)
        slo_w = edi.bitcast(F32).rearrange("p (w t) -> p w t", t=RUN)
        NOH = 4 * RUN
        oh_s = take(NOH * P // 2).bitcast(BF16).rearrange("p (n s) -> p n s", n=NOH)
        ohs = [oh_s[:, i, :] for i in range(NOH)]
        ohm = [take(WM // 2).bitcast(BF16) for _ in range(NOH)]
        x_sb = Ct[:, :, :].rearrange("p a b -> p (a b)")[:, 0:2 * NT * F].bitcast(F32).rearrange("p (t f) -> p t f", t=NT)
        pos[0] = 2 * WS
        Mk = [take(H * NP).rearrange("p (h d) -> p h d", h=H) for _ in range(2)]
        cneg = [take(NP // 2).bitcast(BF16) for _ in range(2)]
        stg = [take(2 * XB) for _ in range(2)]
        WT = [s[:, 0:F] for s in stg]
        stg1 = [s.rearrange("p (a c) -> p a c", a=2) for s in stg]
        pos[0] = 0
        NX = 5
        e1 = [take(2 * DH).rearrange("p (h d) -> p h d", h=2) for _ in range(5)]
        e2 = [take(2 * DH).rearrange("p (h d) -> p h d", h=2) for _ in range(2)]
        xring = [take(XB) for _ in range(NX)]
        hst = take(DT * HF).rearrange("p (t f) -> p t f", t=DT)
        hmn = take(DT * HF).rearrange("p (t f) -> p t f", t=DT)
        abr_at = pos[0]
        abr = take(R * 4 * DH).rearrange("p (r c d) -> p r c d", r=R, c=4)

        def take_r(name, n):
            pos[0] += -pos[0] % 8
            take(n)
            return nc.alloc_sbuf_tensor_at(name, [P, n], F32R, offset=arena_at + (pos[0] - n) * 4)

        WH = KT * HF
        w2raw = cut(abr_at, WH)
        pos[0] = abr_at + WH
        w2_hi, w2_lo = [take_r("w2_hi0", WH)], [take_r("w2_lo0", WH)]
        stg2_at = ARENA - 2 * (HF + 2)
        assert pos[0] <= stg2_at
        stg2 = [cut(stg2_at + i * (HF + 2), HF + 2) for i in range(2)]
        pos[0] = 0
        w2_hi.append(take_r("w2_hi1", WH))
        w2_lo.append(take_r("w2_lo1", WH))
        xt_hi = [take_r(f"xt_hi{i}", F) for i in range(2)]
        xt_lo = [take_r(f"xt_lo{i}", F) for i in range(2)]
        Mk2 = take(R * NP).rearrange("p (h d) -> p h d", h=R)
        cneg2 = [take(NP // 2).bitcast(BF16) for _ in range(2)]
        assert pos[0] <= abr_at
        pos[0] = 0
        GT = 4
        ost = take(GT * F).rearrange("p (t f) -> p t f", t=GT)
        xres = take(GT * F).rearrange("p (t f) -> p t f", t=GT)
        g1 = [take(512) for _ in range(2)]
        g2 = [take(512) for _ in range(2)]
        g_hi = [take_r(f"g_hi{i}", 512) for i in range(2)]
        g_lo = [take_r(f"g_lo{i}", 512) for i in range(2)]
        x_hi = [take_r(f"x_hi{i}", XW + XW % 8) for i in range(2)]
        x_lo = [take_r(f"x_lo{i}", XW + XW % 8) for i in range(2)]
        st6 = take(GT * 12).rearrange("p (t s) -> p t s", t=GT)
        mv = take(GT * 2).rearrange("p (t s) -> p t s", t=GT)
        assert pos[0] <= abr_at
        pos[0] = abr_at
        ab2r = take(R * 2 * 512).rearrange("p (r c d) -> p r c d", r=R, c=2)
        x2ring = [take(XW) for _ in range(NX)]
        assert pos[0] <= stg2_at

        names = """edges_in x_in qv_in bias_in consts x_zero code_ready code_out runs_out ranks row_ready rows_in
        off_ready runs_in run_tr flag_sum flag_tot flag_ready x_tr xt_ready wt_tr wt_ready wq_done wq_ready
        qk_done qk_ready oh c_done c_ready fb_built fb_used fb_done fb_free fb_c fb_evac t_done t_evac
        ones_in mk_step mk_cneg mk_tr mk_red ab_ready ab_tr ab_rows ab_out e_ready e2_free a_ready a_used
        h_sum h_max o_sum h_lin h_exp h_ready h_tr ht_ready o_var o_std o_ready o_out chain pool_ready
        x_hi_ready x2_free xb_ready o_norm x_rest w2_in w2_hi_ready w2_ready xt_hi_ready xt_lo_ready""".split()
        S = {n: sem(n) for n in names}
        w_in = [sem(f"w_in{i}") for i in range(2)]
        xr_out = [sem(f"xr_out{i}") for i in range(2)]
        xr_in = [sem(f"xr_in{i}") for i in range(NX)]
        ab_in = [sem(f"ab_in{i}") for i in range(R)]
        xres_in = sem("xres_in")

        class Layer:
            pass

        def layer(H, qv, wqk, qk, ks, mk, mx, ab, C, abd, n):
            v = Layer()
            v.H, v.qv, v.wqk, v.qk, v.ks, v.mk, v.mx, v.ab, v.C, v.abd, v.n = H, qv, wqk, qk, ks, mk, mx, ab, C, abd, n
            v.side = H if H > 1 else R
            return v

        L1 = layer(H, qv1, wqk1, qk1t, ks1, mk1, mx1, ab1, QC, ab_d, 0)
        L2 = layer(1, qv2, wqk2, qk2t, ks2, mk2, mx2, ab2, QC2, ab2_d, 1)
        L1.M, L1.cneg, L1.rows = Mk, cneg, Mk[0][:, 0, :]
        L2.M, L2.cneg, L2.rows = [Mk2, Mk2], cneg2, Mk2[:, 0, :]
        WOFF = [0, 3, 6]
        NU = 2 * RS
        W2_AT = [3, 5]
        MK2_AT, AB2_AT = 47, 54
        GROUPS = [(0, 4), (4, 7), (7, 10)]
        BASE = [0, 0, 6]
        NG1 = 4
        NST = NG1 * RS
        RING = NX
        PAIRS = NW // 2
        LOGITS_AT = R * KT + 2
        T_AT = LOGITS_AT + NT
        MAX_AT = 8
        AB_AT = 12
        MK_AT = 5
        HT_AT = [0, 3, 6]
        HT_OUT_AT = [4, 7, 9]
        XG = 4
        NB_X = 3 * KT

        def bank1(g, i):
            return ps[(DT * g + i) % 8]

        def ht_banks(g):
            return bank1(g + 1, DT), bank1(g + 1, DT + 1)

        def bank2(g, i, b):
            return ps[(BASE[g] + 2 * i + b) % 8]

        def group1(g):
            return g % 2, g // 2

        def store_out(sp, g):
            t0, t1 = GROUPS[g]
            for t in range(t0, t1):
                m = TAIL if t == NT - 1 else P
                sp.wait_ge(S["o_ready"], t + 1)
                sp.dma_start(out[t * P:t * P + m, :], ost[0:m, t - t0, :]).then_inc(S["o_out"], 16)

        def weights(n):
            return wslot[n % 2]

        def landed(n):
            return w_in[n % 2], 16 * (n // 2 + 1)

        def used(n):
            lay, r = n // 6, n % 3
            if n % 6 < 3:
                return S["wq_done"], (lay * R + r + 1) * KT
            return S["t_done"], (lay * R + r + 1) * NT

        block = ctx.enter_context(nc.Block())

        @block.sync
        def _(sp):
            for t, a in ((dsti, dst), (srci, src), (eti, etype)):
                sp.dma_start(t[0:EP, :], a.rearrange("(p c) -> p c", p=EP)).then_inc(S["edges_in"], 16)
            for q, k, t in ((q1, k1, qv1), (q2, k2, qv2)):
                h = t.shape[2] // 2
                sp.dma_start(t[:, :, 0:h], q.rearrange("(k p) h -> p k h", p=P), allow_slow_non_contiguous=True).then_inc(S["qv_in"], 16)
                sp.dma_start(t[:, :, h:2 * h], k.rearrange("(k p) h -> p k h", p=P), allow_slow_non_contiguous=True).then_inc(S["qv_in"], 16)
            sp.wait_ge(S["code_ready"], 1)
            sp.dma_start(code_d[0:E].rearrange("(p c) -> p c", p=EP), code[0:EP, :]).then_inc(S["code_out"], 16)
            sp.dma_start(code_d[E:E + PADL].rearrange("(a c) -> a c", a=1), f1[0:1, 0:PADL]).then_inc(S["code_out"], 16)
            sp.wait_ge(S["code_out"], 32)
            every = bass.AP(code_d.tensor, 0, [[GRAN, NROW], [1, RUNL]])
            sp.dma_start(runs_d[:, :], every).then_inc(S["runs_out"], 16)
            sp.wait_ge(S["x_zero"], 1)
            sp.wait_ge(S["rows_in"], 32)
            sp.dma_start(x_sb[:, 0:XG, :], x[0:XG * P, :].rearrange("(t p) f -> p t f", p=P)).then_inc(S["x_in"], 16)
            sp.wait_ge(S["runs_in"], 32)
            sp.dma_start(x_sb[:, XG:NT - 1, :], x[XG * P:(NT - 1) * P, :].rearrange("(t p) f -> p t f", p=P)).then_inc(S["x_rest"], 16)
            sp.dma_start(x_sb[0:TAIL, NT - 1, :], x[(NT - 1) * P:N, :]).then_inc(S["x_rest"], 16)

            def load_w(n):
                if n >= 2:
                    sp.wait_ge(*used(n - 2))
                w = (W1, W1, W2)[n // 3][n % 3]
                sp.dma_start(weights(n), w.rearrange("(k p) f -> p k f", p=P)).then_inc(w_in[n % 2], 16)

            def load_w2(h):
                if h:
                    sp.wait_ge(S["w2_ready"], 2 * h)
                w = W2[h // 2].rearrange("(k p) f -> p k f", p=P)[:, :, (h % 2) * HF:(h % 2 + 1) * HF]
                sp.dma_start(w2raw.rearrange("p (k f) -> p k f", k=KT), w).then_inc(S["w2_in"], 16)

            load_w(0)
            load_w(1)
            for t, a in ((b1b, b1), (b2b, b2)):
                sp.dma_start(t[:, :], a.rearrange("(a f) -> a f", a=1).broadcast_to([P, F])).then_inc(S["bias_in"], 16)
            for n in range(2, 5):
                load_w(n)

            for n in range(RS):
                sp.wait_ge(S["t_evac"], n + 1)
                sp.dma_start(xr_d[n].rearrange("a p c -> p a c"), stg1[n % 2]).then_inc(xr_out[n % 2], 16)
                if n % NT == NT - 1:
                    load_w(5 + n // NT)

            def ab_store(lay):
                sp.wait_ge(S["ab_rows"], lay.n + 1)
                sp.dma_start(lay.abd[:, :], lay.rows[0:lay.C, :]).then_inc(S["ab_out"], 16)
                sp.wait_ge(S["ab_out"], 16 * (lay.n + 1))

            load_w(8)
            ab_store(L1)
            for i in range(2):
                sp.wait_ge(xr_out[i], 16 * RS // 2)

            def load_ab1(g, r):
                hp, dh = group1(g)
                c = r * 8 + hp * 4
                sp.dma_start(abr[:, r, :, :], ab_d[c:c + 4, dh * DH:(dh + 1) * DH].partition_broadcast(P)).then_inc(ab_in[r], 16)

            for r in range(R):
                if r == R - 1:
                    sp.wait_ge(*used(8))
                load_ab1(0, r)
            for g in range(NG1):
                hp, dh = group1(g)
                for r in range(R):
                    with sp.Fori(0, NT // NX) as j:
                        for i in range(NX):
                            sp.wait_ge(S["a_used"], j * NX + ((g * R + r) * NT + i + 1))
                            sp.dma_start(xring[i], xr_d[bass.ds(j * NX + (r * NT + i), 1), hp].squeeze(0)).then_inc(xr_in[i], 16)
                    sp.wait_ge(S["e_ready"], (g * R + r + 1) * NT)
                    if g + 1 < NG1:
                        load_ab1(g + 1, r)
                    elif r == 0:
                        load_w2(0)
            def load_ab2(g, r):
                t0, t1 = GROUPS[g]
                w = (t1 - t0) * P
                sp.dma_start(ab2r[:, r, :, 0:w], ab2_d[r * 2:r * 2 + 2, t0 * P:t1 * P].partition_broadcast(P)).then_inc(ab_in[r], 16)

            load_w2(1)
            for u in range(NU):
                n, b = u // (2 * NT) * NT + u % NT, u // NT % 2
                sp.wait_ge(S["t_evac"], RS + u + 1)
                w = HF + 2 - 2 * b
                sp.dma_start(xr2_d[n][:, b * (HF + 2):b * (HF + 2) + w], stg2[u % 2][:, 0:w]).then_inc(xr_out[u % 2], 16)
                if u % NT == W2_AT[-1] + 1 and u // NT + 2 < 2 * R:
                    load_w2(u // NT + 2)
                if u == AB2_AT + 1:
                    ab_store(L2)
                    for r in range(R):
                        load_ab2(0, r)
                if u == NU - 4:
                    for i in range(2):
                        sp.wait_ge(xr_out[i], 16 * (RS // 2 + NT))
                    for i in range(NX):
                        sp.dma_start(x2ring[i], xr2_d[i]).then_inc(xr_in[i], 16)

            def load_x(g):
                for t in range(*GROUPS[g]):
                    m = TAIL if t == NT - 1 else P
                    sp.dma_start(xres[0:m, t - GROUPS[g][0], :], x[t * P:t * P + m, :]).then_inc(xres_in, 16)

            for g, (t0, t1) in enumerate(GROUPS):
                for r in range(R):
                    if (g, r) == (0, 1):
                        for i in range(2):
                            sp.wait_ge(xr_out[i], 16 * (RS // 2 + NU // 2))
                    with sp.Fori(1 if (g, r) == (0, 0) else 0, NT // NX) as j:
                        for i in range(NX):
                            sp.wait_ge(S["x2_free"], j * NX + ((g * R + r) * NT + i + 1))
                            sp.dma_start(x2ring[i], xr2_d[bass.ds(j * NX + (r * NT + i), 1)].squeeze(0)).then_inc(xr_in[i], 16)
                    if g + 1 < len(GROUPS):
                        sp.wait_ge(S["e_ready"], NST + (g * R + r + 1) * NT)
                        load_ab2(g + 1, r)
                    if r == 0:
                        if g:
                            sp.wait_ge(S["o_sum"], t0)
                        else:
                            sp.wait_ge(S["t_done"], RS + NU)
                        load_x(g)
                    if r == 1 and g:
                        store_out(sp, g - 1)
            store_out(sp, len(GROUPS) - 1)
            sp.wait_ge(S["o_out"], 16 * NT)

        @block.gpsimd
        def _(pool):
            nc.gpsimd.memset(ident[:, :], 0.0).then_inc(S["pool_ready"], 1)
            pool.wait_ge(S["pool_ready"], 1)
            io = dict(allow_small_or_imprecise_dtypes=True)
            nc.gpsimd.affine_select(out=ident[:, :], in_=ident[:, :], compare_op=ALU.not_equal, fill=1.0,
                                    base=0, pattern=[[-1, P]], channel_multiplier=1).then_inc(S["consts"], 1)
            nc.gpsimd.iota(wrow, [[1, NW]], base=0, channel_multiplier=0, **io).then_inc(S["consts"], 1)
            nc.gpsimd.iota(small[:, 0:2], [[SW, 2]], base=0, channel_multiplier=1, **io).then_inc(S["consts"], 1)
            nc.gpsimd.memset(onesf[:, :], 1.0).then_inc(S["consts"], 1)
            nc.gpsimd.iota(wid, [[SW, 2], [0, RUN], [1, SW]], base=0, channel_multiplier=0, **io).then_inc(S["consts"], 1)
            nc.gpsimd.iota(i_m[:, :], [[1, WM]], base=0, channel_multiplier=0, **io).then_inc(S["consts"], 1)
            nc.gpsimd.iota(i_s[:, :], [[1, P]], base=0, channel_multiplier=0, **io).then_inc(S["consts"], 1)
            nc.gpsimd.memset(zm[:, :], 0.0).then_inc(S["consts"], 1)
            pool.wait_ge(S["code_out"], 32)
            pool.wait_ge(S["row_ready"], 1)
            for s in range(2):
                nc.gpsimd.indirect_dma_start(rowb[0:SW, s, :], None, code_d[0:E].rearrange("(p c) -> p c", c=EC),
                                             bass.IndirectOffsetOnAxis(smalli[0:SW, s:s + 1], 0)).then_inc(S["rows_in"], 16)
            pool.wait_ge(S["off_ready"], 1)
            pool.wait_ge(S["runs_out"], 16)
            for s in range(2):
                nc.gpsimd.indirect_dma_start(runb[0:SW, s, :], None, runs_d[:, :],
                                             bass.IndirectOffsetOnAxis(smalli[0:SW, 2 + s:3 + s], 0)).then_inc(S["runs_in"], 16)
            pool.wait_ge(S["wq_done"], R * KT)
            for s in range(2):
                nc.gpsimd.memset(stg1[s].rearrange("p a (h c) -> p a h c", h=2)[:, :, :, HD], 1.0).then_inc(S["ones_in"], 1)
            for g in range(NG1 - 1):
                pool.wait_ge(S["h_sum"], DT * (g + 1))
                nc.gpsimd.tensor_scalar(hmn, hst, 0.0, None, ALU.min).then_inc(S["h_lin"], 1)
                nc.gpsimd.tensor_scalar(hst, hst, 0.0, -1.0, ALU.max, ALU.add).then_inc(S["h_max"], 1)
                pool.wait_ge(S["h_max"], g + 1)
                pool.wait_ge(S["h_exp"], g + 1)
                nc.gpsimd.tensor_tensor(hst, hst, hmn, ALU.add).then_inc(S["h_ready"], 1)
            pool.wait_ge(S["h_tr"], 3 * NG1)
            for s in range(2):
                nc.gpsimd.memset(stg2[s][:, HF:HF + 2], 1.0).then_inc(S["ones_in"], 1)
            pool.wait_ge(S["bias_in"], 32)

            for g, (t0, t1) in enumerate(GROUPS):
                pool.wait_ge(xres_in, 16 * t1)
                for t in range(t0, t1):
                    m = TAIL if t == NT - 1 else P
                    nc.gpsimd.tensor_tensor(xres[0:m, t - t0, :], xres[0:m, t - t0, :], b2b[0:m, :], ALU.add).then_inc(S["xb_ready"], 1)

        @block.scalar
        def _(act):
            copy = ACT.Copy
            n = 0
            for t0 in range(0, NT, XG):
                for kt in range(KT):
                    w = min(XG, NT - t0) * P
                    act.wait_ge(S["x_tr"], n + 1)
                    nc.scalar.activation(xT[:, kt, t0 * P:t0 * P + w], ps[n % 2][:, 0:w], copy).then_inc(S["xt_ready"], 1)
                    n += 1

            def wq_out(lay, i):
                act.wait_ge(S["wq_done"], lay.n * R * KT + i + 1)
                r, kt = i // KT, i % KT
                o = lay.wqk[:, kt, :].rearrange("p (a r h) -> p a r h", a=2, r=R)[:, :, r, :]
                nc.scalar.activation(o, ps[6 + i % 2][:, 0:2 * lay.H].rearrange("p (a h) -> p a h", a=2), copy).then_inc(S["wq_ready"], 1)

            def wt_out(lay, i):
                act.wait_ge(S["wt_tr"], lay.n * R * KT + i + 1)
                if i >= 2:
                    act.wait_ge(S["wq_done"], lay.n * R * KT + i - 1)
                for b in range(2):
                    last = nc.scalar.activation(WT[i % 2][:, b * HF:(b + 1) * HF], ps[2 + 2 * (i % 2) + b][:, 0:HF], copy)
                last.then_inc(S["wt_ready"], 1)

            def logits(lay):
                act.wait_ge(S["qk_done"], (lay.n + 1) * NT)
                v = ps[6][:, 0:NT * lay.C].rearrange("p (t c) -> p t c", t=NT)
                nc.scalar.activation(lay.qk[:, :, :], v, copy)
                nc.scalar.activation(lay.ks[:, :, :], v[:, :, lay.C // 2:], copy, scale=SLOPE).then_inc(S["qk_ready"], 1)

            def transform_out(n):
                if n == 0:
                    act.wait_ge(S["ones_in"], 2)
                act.wait_ge(S["t_done"], n + 1)
                if n >= 2:
                    act.wait_ge(xr_out[n % 2], 16 * (n // 2))
                for b in range(2):
                    o = stg1[n % 2][:, b, :].rearrange("p (h c) -> p h c", h=2)[:, :, 0:HD]
                    last = nc.scalar.activation(o, ps[2 + 2 * (n % 2) + b][:, 0:HF].rearrange("p (h c) -> p h c", h=2), copy)
                last.then_inc(S["t_evac"], 1)

            act.sem_inc(S["c_ready"], 2)
            for pair in range(PAIRS):
                act.wait_ge(S["c_done"], pair + 3)
                for c in range(2):
                    d = (2 * pair + c) * WIN
                    last = nc.scalar.activation(Ct[:, :, d:d + WIN], ps[pair % 2][:, c * WM:(c + 1) * WM].rearrange("p (a b) -> p a b", b=WIN), copy)
                last.then_inc(S["c_ready"], 1)
                k = pair - 1
                if 0 <= k < R * KT:
                    wt_out(L1, k)
                if 0 <= k - 2 < R * KT:
                    wq_out(L1, k - 2)
                if k == T_AT - 1:
                    logits(L1)
                if k >= T_AT and (k - T_AT) % KT == KT - 1:
                    transform_out((k - T_AT) // KT)

            def ab_rows(lay):
                act.wait_ge(S["ab_tr"], lay.n + 1)
                for b in range(3):
                    w = min(512, NP - 512 * b)
                    last = nc.scalar.activation(lay.rows[0:lay.C, b * 512:b * 512 + w], ps[(0, 1, 6)[b]][0:lay.C, 0:w], copy)
                last.then_inc(S["ab_rows"], 1)

            for n in range((PAIRS - 1 - T_AT) // KT, RS):
                transform_out(n)
            for i in range(2):
                act.wait_ge(xr_out[i], 16 * RS // 2)
            for i in range(R * KT + 1):
                if i < R * KT:
                    wt_out(L2, i)
                if i:
                    wq_out(L2, i - 1)
                if i == AB_AT + 1:
                    ab_rows(L1)

            def ht_out(g, c):
                hp, dh = group1(g)
                a, b = ht_banks(g)
                act.wait_ge(S["h_tr"], 3 * g + c + 1)
                nc.scalar.activation(xT[:, hp * 3 + c, dh * DH:dh * DH + 512], a[:, :], copy)
                nc.scalar.activation(xT[:, hp * 3 + c, dh * DH + 512:(dh + 1) * DH], b[:, 0:DH - 512], copy).then_inc(S["ht_ready"], 1)

            def exp_min(g):
                act.wait_ge(S["h_lin"], g + 1)
                nc.scalar.activation(hmn, hmn, ACT.Exp).then_inc(S["h_exp"], 1)

            for g in range(NG1):
                hp, dh = group1(g)
                for r in range(R):
                    act.wait_ge(ab_in[r], 16 * (g + 1))
                    for t in range(NT):
                        step = g * RS + r * NT + t
                        act.wait_ge(S["a_used"], step + 1)
                        act.wait_ge(S["e2_free"], step + 1)
                        for h in range(2):
                            col = r * H + hp * 2 + h
                            nc.scalar.activation(e1[t % 5][:, h, :], abr[:, r, h, :], ACT.Exp, bias=qk1t[:, t, col + R * H:col + R * H + 1])
                            last = nc.scalar.activation(e2[t % 2][:, h, :], abr[:, r, 2 + h, :], ACT.Exp, bias=ks1[:, t, col:col + 1])
                        last.then_inc(S["e_ready"], 1)
                        if (r, t) == (0, 7) and g:
                            exp_min(g - 1)
                        if r == R - 1 and t in HT_OUT_AT and g:
                            ht_out(g - 1, HT_OUT_AT.index(t))

            def w2_upper(h, i):
                o = slice(i * WH // 2, (i + 1) * WH // 2)
                act.wait_ge(S["w2_in"], 16 * (h + 1))
                if h >= 2:
                    act.wait_ge(S["t_done"], RS + (h - 1) * NT)
                nc.scalar.activation(w2_hi[h % 2][:, o], w2raw[:, o], copy).then_inc(S["w2_hi_ready"], 1)

            def xt_upper(u):
                if u >= 2:
                    act.wait_ge(S["t_done"], RS + u - 1)
                t = u % NT
                nc.scalar.activation(xt_hi[u % 2][:, :].rearrange("p (k s) -> p k s", k=KT), xT[:, :, t * P:(t + 1) * P], copy).then_inc(S["xt_hi_ready"], 1)

            def unit_out(u):
                act.wait_ge(S["t_done"], RS + u + 1)
                if u == 0:
                    act.wait_ge(S["ones_in"], 4)
                if u >= 2:
                    act.wait_ge(xr_out[u % 2], 16 * (RS // 2 + u // 2))
                nc.scalar.activation(stg2[u % 2][:, 0:HF], ps[2 + u % 2][:, 0:HF], copy).then_inc(S["t_evac"], 1)

            for i in range(2):
                w2_upper(0, i)
            for c in range(3):
                act.wait_ge(S["h_lin"], NG1 + c)
                nc.scalar.activation(hmn[:, :, c * P:(c + 1) * P], hmn[:, :, c * P:(c + 1) * P], ACT.Exp).then_inc(S["h_exp"], 1)
            for c in range(3):
                ht_out(NG1 - 1, c)
            act.wait_ge(S["ht_ready"], 3 * NG1)
            xt_upper(0)
            xt_upper(1)
            logits(L2)
            for u in range(2, NU + 1):
                if u < NU:
                    xt_upper(u)
                    if u % NT in W2_AT and u // NT + 1 < 2 * R:
                        w2_upper(u // NT + 1, W2_AT.index(u % NT))
                if u == 2:
                    unit_out(0)
                unit_out(u - 1)
                if u == AB2_AT + 1:
                    ab_rows(L2)

            def deviations(g, i0, i1):
                act.wait_ge(S["o_var"], GROUPS[g][0] + i1)
                nc.scalar.activation(mv[:, i0:i1, 1], mv[:, i0:i1, 1], ACT.Sqrt).then_inc(S["o_std"], i1 - i0)

            def normalise(g, i):
                t = GROUPS[g][0] + i
                act.wait_ge(S["o_norm"], t + 1)
                nc.scalar.activation(ost[:, i, :], ost[:, i, :], ACT.Identity, bias=mv[:, i, 0:1], scale=mv[:, i, 1:2]).then_inc(S["o_ready"], 1)

            for g, (t0, t1) in enumerate(GROUPS):
                w = (t1 - t0) * P
                for r in range(R):
                    act.wait_ge(ab_in[r], 16 * (NG1 + g + 1))
                    for t in range(NT):
                        step = NST + g * RS + r * NT + t
                        act.wait_ge(S["e2_free"], step + 1)
                        nc.scalar.activation(g1[t % 2][:, 0:w], ab2r[:, r, 0, 0:w], ACT.Exp, bias=qk2t[:, t, R + r:R + r + 1])
                        nc.scalar.activation(g2[t % 2][:, 0:w], ab2r[:, r, 1, 0:w], ACT.Exp, bias=ks2[:, t, r:r + 1]).then_inc(S["e_ready"], 1)
                        act.wait_ge(xr_in[t % NX], 16 * (step // NX + 1))
                        act.wait_ge(S["a_used"], RING + step - 1)
                        nc.scalar.activation(x_hi[t % 2][:, 0:XW], x2ring[t % NX], copy).then_inc(S["x_hi_ready"], 1)
                        if (r, t) == (1, 0) and g:
                            deviations(g - 1, 0, GROUPS[g - 1][1] - GROUPS[g - 1][0])
                        if r == 1 and g and 0 <= t - 4 < GROUPS[g - 1][1] - GROUPS[g - 1][0]:
                            normalise(g - 1, t - 4)
            g, n = len(GROUPS) - 1, GROUPS[-1][1] - GROUPS[-1][0]
            for i in range(n):
                deviations(g, i, i + 1)
                if i:
                    normalise(g, i - 1)
            normalise(g, n - 1)

        @block.tensor
        def _(pe):
            mm = nc.tensor.matmul
            pe.wait_ge(S["consts"], 8)
            pe.wait_ge(S["ranks"], 1)
            for s in range(2):
                last = mm(ps[7][0:SW, s:s + 1], G[0:EP, s * SW:(s + 1) * SW], onesf[0:EP, 0:1], start=True, stop=True)
            last.then_inc(S["ranks"], 1)
            n = 0
            for t0 in range(0, NT, XG):
                if t0 == 0:
                    pe.wait_ge(S["x_in"], 16)
                if t0 == XG:
                    pe.wait_ge(S["runs_in"], 32)
                    for s in range(2):
                        for t in range(RUN):
                            c = (s * RUN + t) * SW
                            last = nc.tensor.transpose(ps[7][:, c:c + SW], runb[0:SW, s, t * P:(t + 1) * P], ident[0:SW, 0:SW])
                    last.then_inc(S["run_tr"], 1)
                    pe.wait_ge(S["x_rest"], 32)
                for kt in range(KT):
                    if n >= 2:
                        pe.wait_ge(S["xt_ready"], n - 1)
                    for t in range(t0, min(t0 + XG, NT)):
                        last = nc.tensor.transpose(ps[n % 2][:, (t - t0) * P:(t - t0 + 1) * P], x_sb[:, t, kt * P:(kt + 1) * P], ident[:, :])
                    last.then_inc(S["x_tr"], 1)
                    n += 1

            def wt_transposes(lay, i):
                r, kt = i // KT, i % KT
                n = WOFF[2 * lay.n] + r
                if kt == 0:
                    pe.wait_ge(*landed(n))
                if i >= 2:
                    pe.wait_ge(S["wt_ready"], lay.n * R * KT + i - 1)
                elif lay is L2:
                    pe.wait_ge(S["t_evac"], RS)
                for ft in range(KT):
                    last = nc.tensor.transpose(ps[2 + 2 * (i % 2) + ft // 3][:, (ft % 3) * P:(ft % 3 + 1) * P],
                                               weights(n)[:, kt, ft * P:(ft + 1) * P], ident[:, :])
                last.then_inc(S["wt_tr"], 1)

            def wq_product(lay, i):
                pe.wait_ge(S["wt_ready"], lay.n * R * KT + i + 1)
                if i >= 2:
                    pe.wait_ge(S["wq_ready"], lay.n * R * KT + i - 1)
                elif lay is L1:
                    pe.wait_ge(S["flag_ready"], 1)
                    pe.wait_ge(S["qv_in"], 64)
                else:
                    pe.wait_ge(S["mk_red"], NT)
                for ft in range(KT):
                    last = mm(ps[6 + i % 2][:, 0:2 * lay.H], WT[i % 2][:, ft * P:(ft + 1) * P], lay.qv[:, ft, :],
                              start=ft == 0, stop=ft == KT - 1)
                last.then_inc(S["wq_done"], 1)

            def logits(lay, t):
                if t == 0:
                    pe.wait_ge(S["wq_ready"], (lay.n + 1) * R * KT)
                for kt in range(KT):
                    last = mm(ps[6][:, t * lay.C:(t + 1) * lay.C], xT[:, kt, t * P:(t + 1) * P], lay.wqk[:, kt, :],
                              start=kt == 0, stop=kt == KT - 1)
                last.then_inc(S["qk_done"], 1)

            def transform_tile(r, t, kt):
                i = r * NT + t
                if kt == 0:
                    if t == 0:
                        pe.wait_ge(*landed(WOFF[1] + r))
                    if i >= 2:
                        pe.wait_ge(S["t_evac"], i - 1)
                    else:
                        pe.wait_ge(S["wt_ready"], R * KT)
                for b in range(2):
                    last = mm(ps[2 + 2 * (t % 2) + b][:, 0:HF], xT[:, kt, t * P:(t + 1) * P],
                              weights(WOFF[1] + r)[:, kt, b * HF:(b + 1) * HF], start=kt == 0, stop=kt == KT - 1)
                if kt == KT - 1:
                    last.then_inc(S["t_done"], 1)

            def transform(r, t0=0):
                for t in range(t0, NT):
                    for kt in range(KT):
                        transform_tile(r, t, kt)

            def unit(u):
                h = u // NT
                if u % NT == 0:
                    pe.wait_ge(S["w2_ready"], 2 * (h + 1))
                pe.wait_ge(S["xt_lo_ready"], u + 1)
                if u >= 2:
                    pe.wait_ge(S["t_evac"], RS + u - 1)
                for kt in range(KT):
                    for n, (a, w) in enumerate(((xt_hi, w2_hi), (xt_hi, w2_lo), (xt_lo, w2_hi))):
                        last = mm(ps[2 + u % 2][:, 0:HF], a[u % 2][:, kt * P:(kt + 1) * P], w[h % 2][:, kt * HF:(kt + 1) * HF],
                                  start=kt == 0 and n == 0, stop=kt == KT - 1 and n == 2)
                last.then_inc(S["t_done"], 1)

            pe.wait_ge(S["flag_sum"], 1)
            mm(ps[7][0:1, 0:1], small[:, 8:9], onesf[:, 0:1], start=True, stop=True).then_inc(S["flag_tot"], 1)
            pe.sem_inc(S["c_done"], 2)
            pe.wait_ge(S["xt_ready"], NB_X)
            for pair in range(PAIRS):
                h = pair % 2
                pe.wait_ge(S["oh"], pair + 1)
                pe.wait_ge(S["c_ready"], pair + 1)
                for c in range(2):
                    for t in range(RUN):
                        n = (h * 2 + c) * RUN + t
                        last = mm(ps[h][:, c * WM:(c + 1) * WM], ohs[n], ohm[n], start=t == 0, stop=t == RUN - 1)
                last.then_inc(S["c_done"], 1)
                if pair < R * KT:
                    wt_transposes(L1, pair)
                if 0 <= pair - 2 < R * KT:
                    wq_product(L1, pair - 2)
                if LOGITS_AT <= pair < T_AT:
                    logits(L1, pair - LOGITS_AT)
                if pair >= T_AT:
                    transform_tile(0, (pair - T_AT) // KT, (pair - T_AT) % KT)
            pe.wait_ge(S["flag_ready"], 1)
            held = pe.value_load(smalli[0:1, 4:5], min_val=0, max_val=E)
            with pe.If(held < E):
                pe.wait_ge(S["c_ready"], NW // 2 + 2)
                with pe.Fori(0, NW) as w:
                    pe.wait_ge(S["fb_free"], w + 1)
                    mm(ps[0][:, 0:WM], zm[:, 0:P], zm[:, 0:WM], start=True, stop=False, skip_group_check=True)
                    with pe.Fori(0, EC // 4) as j:
                        pe.wait_ge(S["fb_built"], w * (EC // 4) + j + 1)
                        for t in range(4):
                            last = mm(ps[0][:, 0:WM], ohs[t][0:EP, :], ohm[t][0:EP, :], start=False, stop=True, skip_group_check=True)
                        last.then_inc(S["fb_used"], 1)
                    last = mm(ps[0][:, 0:WM], zm[:, 0:P], zm[:, 0:WM], start=False, stop=True, skip_group_check=True)
                    last.then_inc(S["fb_done"], 1)
                pe.wait_ge(S["fb_evac"], NW)

            def mk_transpose(lay, u, t):
                u0 = u if lay is L1 else R
                if t == 0:
                    pe.wait_ge(S["mk_step"], (u + 1) * NT * H if lay is L1 else RS * (H + 1))
                i = u0 * NT + t
                if i >= 2:
                    pe.wait_ge(S["mk_red"], i - 1)
                for c in range(lay.side):
                    last = nc.tensor.transpose(ps[6 + i % 2][:, c * P:(c + 1) * P], lay.M[u0 % 2][:, c, t * P:(t + 1) * P], ident[:, :])
                last.then_inc(S["mk_tr"], 1)

            def mk_transposes(lay, u):
                for t in range(NT):
                    mk_transpose(lay, u, t)

            def ab_transposes(lay, wq):
                pe.wait_ge(S["ab_ready"], lay.n + 1)
                pe.wait_ge(S["wq_ready"], wq)
                for t in range(NT):
                    last = nc.tensor.transpose(ps[(0, 1, 6)[t // 4]][0:lay.C, (t % 4) * P:(t % 4 + 1) * P], lay.ab[:, t, :], ident[:, :])
                last.then_inc(S["ab_tr"], 1)

            for kt in range((PAIRS - T_AT) % KT, KT) if (PAIRS - T_AT) % KT else ():
                transform_tile(0, (PAIRS - T_AT) // KT, kt)
            transform(0, -(-(PAIRS - T_AT) // KT))
            transform(1)
            for t in range(NT):
                for kt in range(KT):
                    n = (t - MK_AT) * KT + kt
                    if 0 <= n < NT:
                        mk_transpose(L1, 0, n)
                    transform_tile(2, t, kt)
            wt_transposes(L2, 0)
            for i in range(R * KT):
                if i + 1 < R * KT:
                    wt_transposes(L2, i + 1)
                if i > MAX_AT:
                    pe.wait_ge(S["mk_red"], R * NT)
                if i == AB_AT + 2:
                    pe.wait_ge(S["ab_rows"], 1)
                wq_product(L2, i)
                if i == MAX_AT:
                    pe.wait_ge(S["wq_ready"], R * KT + i + 1)
                    mk_transposes(L1, 1)
                    mk_transposes(L1, 2)
                if i == AB_AT:
                    ab_transposes(L1, R * KT + i + 1)

            def h_transposes(g, c):
                a, b = ht_banks(g)
                pe.wait_ge(S["h_ready"], g + 1 + (c if g == NG1 - 1 else 0))
                if 3 * g + c:
                    pe.wait_ge(S["ht_ready"], 3 * g + c)
                for t in range(DT):
                    last = nc.tensor.transpose((a, b)[t // 4][:, (t % 4) * P:(t % 4 + 1) * P], hst[:, t, c * P:(c + 1) * P], ident[:, :])
                last.then_inc(S["h_tr"], 1)

            pe.sem_inc(S["a_used"], RING)
            pe.wait_ge(S["ab_rows"], 1)
            pe.wait_ge(S["wt_ready"], 2 * R * KT)
            for g in range(NG1):
                if g >= 2:
                    pe.wait_ge(S["ht_ready"], 3 * (g - 1))
                for i in range(DT):
                    if g and i >= 3:
                        pe.wait_ge(S["h_sum"], DT * (g - 1) + i - 2)
                    mm(bank1(g, i)[:, 0:XB], zm[:, 0:P], zm[:, 0:XB], start=True, stop=False, skip_group_check=True)

                def step(r, t):
                    pe.wait_ge(S["a_ready"], r * NT + (g * RS + t + 1))
                    pe.wait_ge(xr_in[t % NX], r * (16 * NT // NX) + 16 * (g * RS // NX + t // NX + 1))
                    for h in range(2):
                        for i in range(DT):
                            o = h * (HD + 1)
                            last = mm(bank1(g, i)[:, o:o + HD + 1], e1[t % 5][:, h, i * P:(i + 1) * P], xring[t % NX][:, o:o + HD + 1],
                                      start=False, stop=True, skip_group_check=True)
                    last.then_inc(S["a_used"], 1)

                with pe.Fori(0, R - 1) as r:
                    for t in range(NT):
                        step(r, t)
                for t in range(NT):
                    if t in HT_AT and g:
                        h_transposes(g - 1, HT_AT.index(t))
                    step(R - 1, t)
            for c in range(3):
                h_transposes(NG1 - 1, c)

            pe.wait_ge(S["ht_ready"], 3 * NG1)
            for t in range(NT):
                logits(L2, t)
            for u in range(NU):
                for t in range(2 * (u - MK2_AT), 2 * (u - MK2_AT) + 2):
                    if 0 <= t < NT:
                        mk_transpose(L2, 0, t)
                if u == AB2_AT:
                    ab_transposes(L2, 2 * R * KT)
                unit(u)
            pe.wait_ge(S["ab_rows"], 2)
            pe.wait_ge(S["t_evac"], RS + NU)
            for g, (t0, t1) in enumerate(GROUPS):
                for i in range(t1 - t0):
                    if g:
                        pe.wait_ge(S["o_sum"], GROUPS[g - 1][0] + (i + 1 if g == 1 else max(i, 1)))
                    for b in range(2):
                        mm(bank2(g, i, b)[:, 0:HF + 2], zm[:, 0:P], zm[:, 0:HF + 2], start=True, stop=False, skip_group_check=True)
                with pe.Fori(0, R) as r:
                    for t in range(NT):
                        pe.wait_ge(S["a_ready"], r * NT + (NST + g * RS + t + 1))
                        for i in range(t1 - t0):
                            for a, x_ in ((g_hi, x_hi), (g_hi, x_lo), (g_lo, x_hi)):
                                for b in range(2):
                                    n = HF + 2 - 2 * b
                                    last = mm(bank2(g, i, b)[:, 0:n], a[t % 2][:, i * P:(i + 1) * P],
                                              x_[t % 2][:, b * (HF + 2):b * (HF + 2) + n], start=False, stop=True, skip_group_check=True)
                        last.then_inc(S["a_used"], 1)

        @block.vector
        def _(dve):
            V = nc.vector
            links = [0]

            def link(ins):
                links[0] += 1
                ins.then_inc(S["chain"], 1)
                dve.wait_ge(S["chain"], links[0])

            V.memset(x_sb[:, NT - 1, :], 0.0).then_inc(S["x_zero"], 1)
            V.memset(f1[0:1, 0:PADL], float(2047 * CODE_DST)).then_inc(S["chain"], 1)
            links[0] += 1
            dve.wait_ge(S["edges_in"], 48)
            link(V.scalar_tensor_tensor(tmpf[0:EP, :], eti[0:EP, :], float(CODE_TYPE), srci[0:EP, :], ALU.mult, ALU.add))
            link(V.scalar_tensor_tensor(code[0:EP, :], dsti[0:EP, :], float(CODE_DST), tmpf[0:EP, :], ALU.mult, ALU.add))
            dve.sem_inc(S["code_ready"], 1)
            dve.wait_ge(S["consts"], 8)
            link(V.tensor_scalar(wrow, wrow, float(WIN * CODE_DST), None, ALU.mult))
            link(V.tensor_scalar(small[:, 2:4], small[:, 0:2], float(WIN * CODE_DST), None, ALU.mult))
            V.tensor_scalar(G[0:EP, :], wrow[0:EP, :], code[0:EP, 0:1], None, ALU.is_gt).then_inc(S["ranks"], 1)
            dve.wait_ge(S["ranks"], 2)
            link(V.tensor_scalar(small[0:SW, 4:6], ps[7][0:SW, 0:2], -1.0, 0.0, ALU.add, ALU.max))
            V.tensor_copy(smalli[0:SW, 0:2], small[0:SW, 4:6]).then_inc(S["row_ready"], 1)
            dve.wait_ge(S["rows_in"], 32)
            for s in range(2):
                link(V.tensor_scalar(tmpf[0:SW, :], rowb[0:SW, s, :], small[0:SW, 2 + s:3 + s], 0.0, ALU.is_lt, ALU.add,
                                     accum_out=small[0:SW, 6 + s:7 + s]))
            link(V.scalar_tensor_tensor(small[0:SW, 10:12], small[0:SW, 4:6], float(EC), small[0:SW, 6:8], ALU.mult, ALU.add))
            link(V.tensor_scalar(small[0:SW, 10:12], small[0:SW, 10:12], float(E - 1), None, ALU.min))
            link(V.tensor_copy(smalli[0:SW, 2:4], small[0:SW, 10:12]))
            V.tensor_scalar(smalli[0:SW, 2:4], smalli[0:SW, 2:4], GRAN.bit_length() - 1, None, ALU.logical_shift_right).then_inc(S["off_ready"], 1)

            def unpack(codes, window, column, source, t0, t1):
                link(V.tensor_scalar(t0, codes, P - 1, None, ALU.bitwise_and))
                link(V.tensor_copy(source, t0))
                link(V.tensor_scalar(t0, codes, 7, 63, ALU.logical_shift_right, ALU.bitwise_and))
                link(V.tensor_scalar(t1, codes, 11, 3, ALU.logical_shift_right, ALU.bitwise_and))
                link(V.scalar_tensor_tensor(column, t1, float(NT - 16), t0, ALU.mult, ALU.add))
                link(V.tensor_scalar(t0, codes, 13, WIN - 1, ALU.logical_shift_right, ALU.bitwise_and))
                link(V.scalar_tensor_tensor(column, column, float(WIN), t0, ALU.mult, ALU.add))
                link(V.tensor_scalar(t0, codes, 16, None, ALU.logical_shift_right))
                link(V.tensor_copy(window, t0))

            dve.wait_ge(S["run_tr"], 1)
            link(V.tensor_copy(edi, ps[7][:, 0:NE]))
            unpack(edi, f0, f1, slo, u0, u1)
            link(V.tensor_tensor(f0, f0, wid, ALU.is_equal))
            link(V.scalar_tensor_tensor(mcode, f1, 1.0, f0, ALU.add, ALU.mult))
            link(V.tensor_scalar(mcode, mcode, -1.0, None, ALU.add))
            link(V.tensor_copy(slo_w.rearrange("p (s w) t -> p s t w", s=2), slo.rearrange("p (s t w) -> p s t w", s=2, t=RUN)))
            V.reduce_sum(small[:, 8:9], f0, AX).then_inc(S["flag_sum"], 1)
            dve.wait_ge(S["flag_tot"], 1)
            V.tensor_copy(smalli[0:1, 4:5], ps[7][0:1, 0:1]).then_inc(S["flag_ready"], 1)
            with dve.Fori(0, 2) as s:
                with dve.Fori(0, SW // 4) as j:
                    for h in range(2):
                        dve.wait_ge(S["c_done"], s * (SW // 2) + j * 2 + (h + 1))
                        w = slo_w[:, bass.ds(s * SW + j * 4 + h * 2, 2), :]
                        V.tensor_tensor(oh_s[:, h * 2 * RUN:(h + 1) * 2 * RUN, :].rearrange("p (c t) s -> p c t s", c=2),
                                        i_s[:, :].unsqueeze(1).unsqueeze(1).broadcast_to([P, 2, RUN, P]),
                                        w.unsqueeze(3).broadcast_to([P, 2, RUN, P]), ALU.is_equal)
                        for c in range(2):
                            for t in range(RUN):
                                col = s * (RUN * SW) + j * 4 + (t * SW + h * 2 + c)
                                last = V.tensor_scalar(ohm[(h * 2 + c) * RUN + t], i_m[:, :], mcode[:, bass.ds(col, 1)], None, ALU.is_equal)
                        last.then_inc(S["oh"], 1)
            dve.wait_ge(S["c_ready"], NW // 2 + 2)
            dve.wait_ge(S["flag_ready"], 1)
            held = dve.value_load(smalli[0:1, 4:5], min_val=0, max_val=E)
            with dve.If(held < E):
                before = links[0]
                nat = edi[0:EP, 0:EC]
                link(V.tensor_copy(nat, code[0:EP, :]))
                unpack(nat, f0[0:EP, 0:EC], f1[0:EP, 0:EC], slo[0:EP, 0:EC], u0[0:EP, 0:EC], u1[0:EP, 0:EC])
                dve.sem_inc(S["fb_used"], 1)
                with dve.Fori(0, NW) as w:
                    dve.sem_inc(S["fb_free"], 1)
                    V.tensor_scalar(wid[0:EP, 0:EC], f0[0:EP, 0:EC], float(WIN * CODE_DST), wrow[0:EP, bass.ds(w, 1)], ALU.mult, ALU.is_equal).then_inc(S["fb_c"], 1)
                    dve.wait_ge(S["fb_c"], w * 2 + 1)
                    V.scalar_tensor_tensor(mcode[0:EP, 0:EC], f1[0:EP, 0:EC], 1.0, wid[0:EP, 0:EC], ALU.add, ALU.mult).then_inc(S["fb_c"], 1)
                    with dve.Fori(0, EC // 4) as j:
                        dve.wait_ge(S["fb_c"], w * 2 + 2)
                        dve.wait_ge(S["fb_used"], w * (EC // 4) + j + 1)
                        for t in range(4):
                            V.tensor_scalar(ohs[t][0:EP, :], i_s[0:EP, :], slo[0:EP, bass.ds(j * 4 + t, 1)], None, ALU.is_equal)
                            last = V.tensor_scalar(ohm[t][0:EP, :], i_m[0:EP, :], 1.0, mcode[0:EP, bass.ds(j * 4 + t, 1)], ALU.add, ALU.is_equal)
                        last.then_inc(S["fb_built"], 1)
                    dve.wait_ge(S["fb_done"], w + 1)
                    V.tensor_copy(Ct[:, :, bass.ds(w * WIN, WIN)], ps[0][:, 0:WM].rearrange("p (a b) -> p a b", b=WIN)).then_inc(S["fb_evac"], 1)
                    dve.wait_ge(S["fb_evac"], w + 1)
                fb_links = links[0] - before
            with dve.Else():
                dve.sem_inc(S["chain"], fb_links)

            def maxima(r):
                m = Mk[r % 2]

                def mask(i):
                    if i >= 2:
                        dve.wait_ge(S["mk_step"], (i - 1) * H)
                    V.tensor_scalar(cneg[i % 2], Ct[:, i, :], 0.0, -BIG, ALU.is_equal, ALU.mult).then_inc(S["mk_cneg"], 1)

                mask(r * NT)
                for t in range(NT):
                    i = r * NT + t
                    if t < NT - 1:
                        mask(i + 1)
                    dve.wait_ge(S["mk_cneg"], i + 1)
                    for h in range(H):
                        k = qk1t[:, t, (R + r) * H + h:(R + r) * H + h + 1]
                        if t == 0:
                            last = V.tensor_scalar(m[:, h, :], cneg[i % 2], k, None, ALU.add)
                        else:
                            dve.wait_ge(S["mk_step"], (i - 1) * H + h + 1)
                            last = V.scalar_tensor_tensor(m[:, h, 0:N], cneg[i % 2][:, 0:N], k, m[:, h, 0:N], ALU.add, ALU.max)
                        last.then_inc(S["mk_step"], 1)

            def reduce(lay, u, t):
                u0 = u if lay is L1 else R
                n = lay.side
                i = u0 * NT + t
                dve.wait_ge(S["mk_tr"], i + 1)
                o = lay.mk[:, t, u, :] if lay is L1 else lay.mk[:, t, :, 0]
                V.reduce_max(o, ps[6 + i % 2][:, 0:n * P].rearrange("p (c s) -> p c s", c=n), AX).then_inc(S["mk_red"], 1)

            def shifts(lay):
                dve.wait_ge(S["mk_red"], (R if lay is L1 else R + 1) * NT)
                H_ = lay.H
                q = lay.qk[:, :, 0:R * H_].rearrange("p t (r h) -> p t r h", r=R)
                k = lay.mk
                m, n, o = lay.mx[:, 0], lay.mx[:, 1], lay.mx[:, 2]
                link(V.tensor_tensor(m, q[:, :, 0, :], k[:, :, 0, :], ALU.add))
                for r in range(1, R):
                    link(V.tensor_tensor(n, q[:, :, r, :], k[:, :, r, :], ALU.add))
                    link(V.tensor_tensor(m, m, n, ALU.max))
                link(V.tensor_scalar(n, m, -BIG / 2, None, ALU.is_gt))
                link(V.scalar_tensor_tensor(o, m, SLOPE, m, ALU.mult, ALU.max))
                link(V.tensor_tensor(m, o, n, ALU.mult))
                w = min(2, H_)
                for r in range(R):
                    for hp in range(H_ // w):
                        c = (r * (H_ // w) + hp) * 2 * w
                        qq, mm_ = q[:, :, r, hp * w:(hp + 1) * w], m[:, :, hp * w:(hp + 1) * w]
                        V.tensor_tensor(lay.ab[:, :, c:c + w], qq, mm_, ALU.subtract)
                        last = V.scalar_tensor_tensor(lay.ab[:, :, c + w:c + 2 * w], qq, SLOPE, mm_, ALU.mult, ALU.subtract)
                last.then_inc(S["ab_ready"], 1)

            dve.wait_ge(S["c_ready"], NW // 2 + 2)
            dve.wait_ge(S["qk_ready"], 1)
            maxima(0)
            maxima(1)
            for t in range(NT):
                reduce(L1, 0, t)
            maxima(2)
            for t in range(NT):
                reduce(L1, 1, t)
            for t in range(NT):
                reduce(L1, 2, t)
            shifts(L1)

            dve.sem_inc(S["e2_free"], 2)
            dve.wait_ge(S["bias_in"], 32)

            def attention1(g, r, t):
                hp, dh = group1(g)
                step = r * NT + (g * RS + t)
                dve.wait_ge(S["e_ready"], step + 1)
                V.tensor_tensor(e1[t % 5], e1[t % 5], e2[t % 2], ALU.max).then_inc(S["e2_free"], 1)
                dve.wait_ge(S["e2_free"], step + 3)
                cc = Ct[:, r * NT + t, dh * DH:(dh + 1) * DH].unsqueeze(1) if isinstance(r, int) else \
                    Ct[:, bass.ds(r * NT + t, 1), dh * DH:(dh + 1) * DH]
                V.scalar_tensor_tensor(e1[t % 5], e1[t % 5], 1.0, cc.broadcast_to([P, 2, DH]), ALU.min, ALU.mult).then_inc(S["a_ready"], 1)

            def rows1(g):
                hp, dh = group1(g)
                dve.wait_ge(S["a_used"], RING + (g + 1) * RS)
                if g:
                    dve.wait_ge(S["h_tr"], 3 * g)
                z = small[:, 16:16 + 2 * DT].rearrange("p (t h) -> p t h", h=2)
                for i in range(DT):
                    last = V.tensor_scalar(z[:, i, :], bank1(g, i)[:, 0:XB].rearrange("p (h c) -> p h c", h=2)[:, :, HD], Z_EPS, None, ALU.add)
                link(last)
                link(V.reciprocal(z, z))
                for i in range(DT):
                    for h in range(2):
                        o = h * (HD + 1)
                        last = V.scalar_tensor_tensor(hst[:, i, h * HD:(h + 1) * HD], bank1(g, i)[:, o:o + HD], z[:, i, h:h + 1],
                                                      b1b[:, hp * HF + h * HD:hp * HF + (h + 1) * HD], ALU.mult, ALU.add)
                    last.then_inc(S["h_sum"], 1)

            for g in range(NG1):
                for t in range(NT):
                    if t == 2 and g:
                        rows1(g - 1)
                    attention1(g, 0, t)
                with dve.Fori(1, R) as r:
                    for t in range(NT):
                        attention1(g, r, t)

            def w2_lower(h, i):
                o = slice(i * WH // 2, (i + 1) * WH // 2)
                dve.wait_ge(S["w2_hi_ready"], 2 * h + i + 1)
                V.tensor_tensor(w2_lo[h % 2][:, o], w2raw[:, o], w2_hi[h % 2][:, o], ALU.subtract).then_inc(S["w2_ready"], 1)

            def xt_lower(u):
                t = u % NT
                dve.wait_ge(S["xt_hi_ready"], u + 1)
                V.tensor_tensor(xt_lo[u % 2][:, :].rearrange("p (k s) -> p k s", k=KT), xT[:, :, t * P:(t + 1) * P],
                                xt_hi[u % 2][:, :].rearrange("p (k s) -> p k s", k=KT), ALU.subtract).then_inc(S["xt_lo_ready"], 1)

            for i in range(2):
                w2_lower(0, i)
            rows1(NG1 - 1)
            dve.wait_ge(S["h_sum"], DT * NG1)
            for c in range(3):
                o = slice(c * P, (c + 1) * P)
                V.tensor_scalar(hmn[:, :, o], hst[:, :, o], 0.0, None, ALU.min).then_inc(S["h_lin"], 1)
            for c in range(3):
                o = slice(c * P, (c + 1) * P)
                link(V.tensor_scalar(hst[:, :, o], hst[:, :, o], 0.0, -1.0, ALU.max, ALU.add))
                dve.wait_ge(S["h_exp"], NG1 + c)
                V.tensor_tensor(hst[:, :, o], hst[:, :, o], hmn[:, :, o], ALU.add).then_inc(S["h_ready"], 1)

            dve.wait_ge(S["h_tr"], 3 * NG1)
            xt_lower(0)
            xt_lower(1)
            dve.wait_ge(S["qk_ready"], 2)

            def mask2(i):
                if i >= 2:
                    dve.wait_ge(S["mk_step"], RS * H + i - 1)
                V.tensor_scalar(cneg2[i % 2], Ct[:, i, :], 0.0, -BIG, ALU.is_equal, ALU.mult).then_inc(S["mk_cneg"], 1)

            def maximum2(i):
                r, t = i // NT, i % NT
                if i == 0:
                    mask2(0)
                if i + 1 < RS:
                    mask2(i + 1)
                dve.wait_ge(S["mk_cneg"], RS + i + 1)
                k = qk2t[:, t, R + r:R + r + 1]
                if t == 0:
                    last = V.tensor_scalar(Mk2[:, r, :], cneg2[i % 2], k, None, ALU.add)
                else:
                    dve.wait_ge(S["mk_step"], RS * H + i)
                    last = V.scalar_tensor_tensor(Mk2[:, r, 0:N], cneg2[i % 2][:, 0:N], k, Mk2[:, r, 0:N], ALU.add, ALU.max)
                last.then_inc(S["mk_step"], 1)

            i = 0
            for u in range(2, NU):
                xt_lower(u)
                if u % NT in W2_AT and u // NT + 1 < 2 * R:
                    w2_lower(u // NT + 1, W2_AT.index(u % NT))
                if u % 3 and i < RS:
                    maximum2(i)
                    i += 1
                if MK2_AT <= u < MK2_AT + NT // 2:
                    for t in range(2):
                        reduce(L2, 0, 2 * (u - MK2_AT) + t)
                if u == MK2_AT + NT // 2:
                    shifts(L2)

            def attention2(g, r, t):
                t0, t1 = GROUPS[g]
                w = (t1 - t0) * P
                step = r * NT + (NST + g * RS + t)
                dve.wait_ge(S["e_ready"], step + 1)
                v = g1[t % 2][:, 0:w]
                link(V.tensor_tensor(v, v, g2[t % 2][:, 0:w], ALU.max))
                cc = Ct[:, r * NT + t, t0 * P:t1 * P]
                link(V.scalar_tensor_tensor(v, v, 1.0, cc, ALU.min, ALU.mult))
                dve.wait_ge(S["a_used"], RING + step - 1)
                hi, lo = g_hi[t % 2][:, 0:w], g_lo[t % 2][:, 0:w]
                V.tensor_copy(hi, v).then_inc(S["chain"], 1)
                links[0] += 1
                dve.wait_ge(S["x_hi_ready"], step - NST + 1)
                V.tensor_tensor(x_lo[t % 2][:, 0:XW], x2ring[t % NX], x_hi[t % 2][:, 0:XW], ALU.subtract).then_inc(S["x2_free"], 1)
                dve.wait_ge(S["chain"], links[0])
                V.tensor_tensor(lo, v, hi, ALU.subtract).then_inc(S["e2_free"], 1)
                dve.wait_ge(S["e2_free"], step + 3)
                dve.sem_inc(S["a_ready"], 1)

            z2 = small[:, 16:16 + GT]

            def rows2(g):
                t0, t1 = GROUPS[g]
                dve.wait_ge(S["a_used"], RING + NST + (g + 1) * RS)
                if g:
                    dve.wait_ge(S["o_out"], 16 * t0)
                for i in range(t1 - t0):
                    last = V.tensor_scalar(z2[:, i:i + 1], bank2(g, i, 0)[:, HF:HF + 1], Z_EPS, None, ALU.add)
                link(last)
                link(V.reciprocal(z2[:, 0:t1 - t0], z2[:, 0:t1 - t0]))
                for i in range(t1 - t0):
                    k = TAIL if t0 + i == NT - 1 else P
                    dve.wait_ge(S["xb_ready"], t0 + i + 1)
                    for b in range(2):
                        last = V.scalar_tensor_tensor(ost[0:k, i, b * HF:(b + 1) * HF], bank2(g, i, b)[0:k, 0:HF], z2[0:k, i:i + 1],
                                                      xres[0:k, i, b * HF:(b + 1) * HF], ALU.mult, ALU.add)
                    last.then_inc(S["o_sum"], 1)
                    if g == len(GROUPS) - 1:
                        statistics(g, i, i + 1)
                        if i:
                            scales(g, i - 1, i)

            def statistics(g, i0, i1):
                dve.wait_ge(S["o_sum"], GROUPS[g][0] + i1)
                for i in range(i0, i1):
                    for b in range(2):
                        last = V.bn_stats(st6[:, i, b * 6:(b + 1) * 6], ost[:, i, b * HF:(b + 1) * HF])
                link(last)
                for i in range(i0, i1):
                    last = V.bn_aggr(mv[:, i, :], st6[:, i, :])
                link(last)
                V.tensor_scalar(mv[:, i0:i1, 1], mv[:, i0:i1, 1], LN_EPS, None, ALU.add).then_inc(S["o_var"], i1 - i0)

            def scales(g, i0, i1):
                dve.wait_ge(S["o_std"], GROUPS[g][0] + i1)
                link(V.reciprocal(mv[:, i0:i1, 1], mv[:, i0:i1, 1]))
                V.scalar_tensor_tensor(mv[:, i0:i1, 0], mv[:, i0:i1, 0], -1.0, mv[:, i0:i1, 1], ALU.mult, ALU.mult).then_inc(S["o_norm"], i1 - i0)

            dve.sem_inc(S["x2_free"], NX)
            for g in range(len(GROUPS)):
                for t in range(NT):
                    if t == 2 and g:
                        rows2(g - 1)
                    attention2(g, 0, t)
                    if t == 6 and g:
                        statistics(g - 1, 0, GROUPS[g - 1][1] - GROUPS[g - 1][0])
                for t in range(NT):
                    attention2(g, 1, t)
                    if t == 2 and g:
                        scales(g - 1, 0, GROUPS[g - 1][1] - GROUPS[g - 1][0])
                for t in range(NT):
                    attention2(g, 2, t)
            rows2(len(GROUPS) - 1)
            scales(len(GROUPS) - 1, GROUPS[-1][1] - GROUPS[-1][0] - 1, GROUPS[-1][1] - GROUPS[-1][0])

_INS = ["x", "src", "dst", "edge_type_3", "L0_gnn_W1", "L0_gnn_q1", "L0_gnn_k1", "L0_gnn_b1",
        "L0_gnn_W2", "L0_gnn_q2", "L0_gnn_k2", "L0_gnn_b2"]


def kernel(**inputs):
    import numpy as _np
    import concourse.bacc as _bacc
    from concourse import mybir as _mybir
    from concourse.bass_utils import run_bass_kernel_spmd as _run

    nc = _bacc.Bacc("TRN2", target_bir_lowering=False, num_devices=1)
    arrays, args = {}, []
    for name in _INS:
        a = _np.ascontiguousarray(inputs[name])
        arrays[f"in_{name}"] = a
        args.append(nc.dram_tensor(f"in_{name}", a.shape, _mybir.dt.from_np(a.dtype), kind="ExternalInput").ap())
    out = nc.dram_tensor("out", inputs["x"].shape, _mybir.dt.float32, kind="ExternalOutput").ap()
    rgat(nc, *args, out)
    r = _run(nc, [arrays], core_ids=[0])
    return r.results[0]["out"]
```
